# Optimizing a Trainium2 kernel written in Bass

```python
import numpy as np
import jax
import jax.numpy as jnp

def _softmax(x, axis=-1):
    return jax.nn.softmax(x, axis=axis)

def _gelu(x):
    return jax.nn.gelu(x, approximate=True)

def _silu(x):
    return jax.nn.silu(x)

def _sigmoid(x):
    return jax.nn.sigmoid(x)

def _layernorm(x, axis=-1, eps=1e-05):
    m = jnp.mean(x, axis=axis, keepdims=True)
    v = jnp.var(x, axis=axis, keepdims=True)
    return (x - m) / jnp.sqrt(v + eps)

def _scatter_add(tgt, idx, src, axis=0):
    return tgt.at[idx].add(src)

def _segment_sum(src, seg, n):
    return jax.ops.segment_sum(src, seg, n)
kernel_name = 'mk_prb_d1_jaxref_r8_7e1719'

def setup_inputs(seed: int=0):
    np.random.seed(seed)
    _w = jnp.asarray

    def _L0_attn_setup():
        import jax, jax.numpy as jnp
        import numpy as np
        import math
        D_MODEL = 128
        N_HEADS = 16
        D_HEAD = D_MODEL // N_HEADS
        WINDOW = 32

        def _attention(x, Wq, bq, Wk, bk, Wv, bv, Wo, bo):
            B, T, C = x.shape
            W = min(WINDOW, T)
            scale = math.sqrt(D_HEAD)

            def proj(Wm, bm):
                return (x @ Wm.T + bm).reshape(B, T, N_HEADS, D_HEAD).transpose(0, 2, 1, 3)
            Q, K, V = (proj(Wq, bq), proj(Wk, bk), proj(Wv, bv))
            scores = jnp.einsum('bhqd,bhkd->bhqk', Q, K) / scale
            idx = jnp.arange(T)
            row = idx[:, None]
            col = idx[None, :]
            allowed = (col <= row) & (row - col < W)
            scores = jnp.where(allowed[None, None], scores, -jnp.inf)
            attn = jax.nn.softmax(scores, axis=-1)
            attn = jnp.nan_to_num(attn, nan=0.0)
            out = jnp.einsum('bhqk,bhkd->bhqd', attn, V)
            out = out.transpose(0, 2, 1, 3).reshape(B, T, C)
            return out @ Wo.T + bo
        key = jax.random.key(seed)
        ks = jax.random.split(key, 9)
        B, T = (2, 256)
        x = jax.random.normal(ks[0], (B, T, D_MODEL), dtype=jnp.float32)
        s = 1.0 / math.sqrt(D_MODEL)
        Wq = jax.random.uniform(ks[1], (D_MODEL, D_MODEL), jnp.float32, -s, s)
        bq = jax.random.uniform(ks[2], (D_MODEL,), jnp.float32, -s, s)
        Wk = jax.random.uniform(ks[3], (D_MODEL, D_MODEL), jnp.float32, -s, s)
        bk = jax.random.uniform(ks[4], (D_MODEL,), jnp.float32, -s, s)
        Wv = jax.random.uniform(ks[5], (D_MODEL, D_MODEL), jnp.float32, -s, s)
        bv = jax.random.uniform(ks[6], (D_MODEL,), jnp.float32, -s, s)
        Wo = jax.random.uniform(ks[7], (D_MODEL, D_MODEL), jnp.float32, -s, s)
        bo = jax.random.uniform(ks[8], (D_MODEL,), jnp.float32, -s, s)
        return {'x': x, 'Wq': Wq, 'bq': bq, 'Wk': Wk, 'bk': bk, 'Wv': Wv, 'bv': bv, 'Wo': Wo, 'bo': bo}
    _L0_attn_in = _L0_attn_setup()

    def _L0_ffn_setup():
        import jax, jax.numpy as jnp
        import numpy as np
        D = 128
        E = 8
        K = 2
        DF = 512
        B, S = (2, 256)
        EPS_LN = 1e-05
        EPS_TOPK = 1e-08

        def _xavier(key, shape, fan_in, fan_out, dtype=jnp.float32):
            bound = float(np.sqrt(6.0 / (fan_in + fan_out)))
            return jax.random.uniform(key, shape, dtype, -bound, bound)
        key = jax.random.key(seed)
        kx, kg, k1, k2 = jax.random.split(key, 4)
        return {'x': jax.random.normal(kx, (B, S, D), jnp.float32), 'gamma': jnp.ones((D,), jnp.float32), 'beta': jnp.zeros((D,), jnp.float32), 'Wg': _xavier(kg, (E, D), D, E), 'bg': jnp.zeros((E,), jnp.float32), 'W1': _xavier(k1, (E, DF, D), D, DF), 'b1': jnp.zeros((E, DF), jnp.float32), 'W2': _xavier(k2, (E, D, DF), DF, D), 'b2': jnp.zeros((E, D), jnp.float32)}
    _L0_ffn_in = _L0_ffn_setup()
    _d = {'L0_attn_x': _L0_attn_in['x'], 'L0_attn_Wq': _L0_attn_in['Wq'], 'L0_attn_bq': _L0_attn_in['bq'], 'L0_attn_Wk': _L0_attn_in['Wk'], 'L0_attn_bk': _L0_attn_in['bk'], 'L0_attn_Wv': _L0_attn_in['Wv'], 'L0_attn_bv': _L0_attn_in['bv'], 'L0_attn_Wo': _L0_attn_in['Wo'], 'L0_attn_bo': _L0_attn_in['bo'], 'L0_ffn_gamma': _L0_ffn_in['gamma'], 'L0_ffn_beta': _L0_ffn_in['beta'], 'L0_ffn_Wg': _L0_ffn_in['Wg'], 'L0_ffn_bg': _L0_ffn_in['bg'], 'L0_ffn_W1': _L0_ffn_in['W1'], 'L0_ffn_b1': _L0_ffn_in['b1'], 'L0_ffn_W2': _L0_ffn_in['W2'], 'L0_ffn_b2': _L0_ffn_in['b2']}
    _x0 = _d['L0_attn_x']
    _d['L0_attn_x'] = jax.random.normal(jax.random.fold_in(jax.random.key(seed), 1), (8, 512, 128), dtype=_x0.dtype)
    del _x0
    return _d

def reference(L0_attn_x, L0_attn_Wq, L0_attn_bq, L0_attn_Wk, L0_attn_bk, L0_attn_Wv, L0_attn_bv, L0_attn_Wo, L0_attn_bo, L0_ffn_gamma, L0_ffn_beta, L0_ffn_Wg, L0_ffn_bg, L0_ffn_W1, L0_ffn_b1, L0_ffn_W2, L0_ffn_b2):

    def _L0_attn_ref(x, Wq, bq, Wk, bk, Wv, bv, Wo, bo):
        import jax, jax.numpy as jnp
        import numpy as np
        import math
        D_MODEL = 128
        N_HEADS = 16
        D_HEAD = D_MODEL // N_HEADS
        WINDOW = 32

        def _attention(x, Wq, bq, Wk, bk, Wv, bv, Wo, bo):
            B, T, C = x.shape
            W = min(WINDOW, T)
            scale = math.sqrt(D_HEAD)

            def proj(Wm, bm):
                return (x @ Wm.T + bm).reshape(B, T, N_HEADS, D_HEAD).transpose(0, 2, 1, 3)
            Q, K, V = (proj(Wq, bq), proj(Wk, bk), proj(Wv, bv))
            scores = jnp.einsum('bhqd,bhkd->bhqk', Q, K) / scale
            idx = jnp.arange(T)
            row = idx[:, None]
            col = idx[None, :]
            allowed = (col <= row) & (row - col < W)
            scores = jnp.where(allowed[None, None], scores, -jnp.inf)
            attn = jax.nn.softmax(scores, axis=-1)
            attn = jnp.nan_to_num(attn, nan=0.0)
            out = jnp.einsum('bhqk,bhkd->bhqd', attn, V)
            out = out.transpose(0, 2, 1, 3).reshape(B, T, C)
            return out @ Wo.T + bo
        return _attention(x, Wq, bq, Wk, bk, Wv, bv, Wo, bo)

    def _L0_ffn_ref(x, gamma, beta, Wg, bg, W1, b1, W2, b2):
        import jax, jax.numpy as jnp
        import numpy as np
        D = 128
        E = 8
        K = 2
        DF = 512
        B, S = (2, 256)
        EPS_LN = 1e-05
        EPS_TOPK = 1e-08

        def _xavier(key, shape, fan_in, fan_out, dtype=jnp.float32):
            bound = float(np.sqrt(6.0 / (fan_in + fan_out)))
            return jax.random.uniform(key, shape, dtype, -bound, bound)
        b, s, d = x.shape
        mu = jnp.mean(x, axis=-1, keepdims=True)
        var = jnp.mean((x - mu) ** 2, axis=-1, keepdims=True)
        xn = (x - mu) / jnp.sqrt(var + EPS_LN) * gamma + beta
        xf = xn.reshape(-1, d)
        logits = xf @ Wg.T + bg
        probs = jax.nn.softmax(logits, axis=-1)
        tp, ti = jax.lax.top_k(probs, K)
        tp = tp / (jnp.sum(tp, axis=-1, keepdims=True) + EPS_TOPK)
        w = jnp.sum(jax.nn.one_hot(ti, E, dtype=xf.dtype) * tp[..., None], axis=1)
        h = jax.nn.gelu(jnp.einsum('td,efd->tef', xf, W1) + b1, approximate=False)
        y = jnp.einsum('tef,edf->ted', h, W2) + b2
        out = jnp.einsum('ted,te->td', y, w)
        return x + out.reshape(b, s, d)
    x = L0_attn_x
    xn = _layernorm(x, axis=-1)
    x = x + _L0_attn_ref(xn, L0_attn_Wq, L0_attn_bq, L0_attn_Wk, L0_attn_bk, L0_attn_Wv, L0_attn_bv, L0_attn_Wo, L0_attn_bo) + _L0_ffn_ref(xn, L0_ffn_gamma, L0_ffn_beta, L0_ffn_Wg, L0_ffn_bg, L0_ffn_W1, L0_ffn_b1, L0_ffn_W2, L0_ffn_b2)
    return x

_drawn_inputs = setup_inputs


def setup_inputs(seed=0):
    import zlib

    import numpy as np

    out = dict(_drawn_inputs(seed))
    spreads = {'L0_ffn_gamma': (1.0, 0.2),
     'L0_ffn_beta': (0.0, 0.1),
     'L0_ffn_bg': (0.0, 0.1),
     'L0_ffn_b1': (0.0, 0.1),
     'L0_ffn_b2': (0.0, 0.1)}
    factors = {'L0_attn_Wq': 4.99,
     'L0_attn_bq': 8.0,
     'L0_attn_Wk': 4.969,
     'L0_attn_bk': 8.0,
     'L0_attn_bv': 3.756}
    for name, (base, spread) in spreads.items():
        noise = np.random.default_rng([zlib.crc32(name.encode()), seed]).standard_normal(out[name].shape)
        drawn = base * np.exp(spread * noise) if base else spread * noise
        out[name] = jnp.asarray(drawn.astype(out[name].dtype))
    for name, factor in factors.items():
        out[name] = (out[name] * factor).astype(out[name].dtype)
    return out
```

```python
from contextlib import ExitStack

import concourse.bass as bass
from concourse import mybir

F32 = mybir.dt.float32
BF16 = mybir.dt.bfloat16
I32 = mybir.dt.int32
ALU = mybir.AluOpType
ACT = mybir.ActivationFunctionType
AX = mybir.AxisListType

P = 128
NEG = -1.0e30
EPS_LN = 1e-5
EPS_TOPK = 1e-8


def attention_and_experts(nc, x, w_attn, b_cols, bias_rows, w_gate, w1, w2, out):
    B, S, D = x.shape
    TB = S // P
    NT = B * TB
    TOKENS = NT * P
    E = w_gate.shape[1]
    DF = w1.shape[1] // E
    FC = DF // P
    DH = 8
    QB = 32
    NQ = S // QB
    G = 4
    SLOT_TILES = 2 * NT + E
    SLOTS = SLOT_TILES * P
    ROW = D + 2
    RING = 4
    NB = bias_rows.shape[1]
    O_B1, O_B2 = 0, E * DF
    O_BO, O_BV, O_BG = O_B2 + E * D, O_B2 + E * D + D, O_B2 + E * D + 2 * D
    NBC = NB // P

    xg_dram = nc.dram_tensor("slot_rows", (SLOTS, ROW), F32, kind="Internal").ap()
    y_dram = nc.dram_tensor("expert_rows", (2 * TOKENS, D), F32, kind="Internal").ap()
    b3_dram = nc.dram_tensor("bias_parts", (3, NB), BF16, kind="Internal").ap()

    with ExitStack() as ctx:
        def sb(name, shape, dt=F32):
            return ctx.enter_context(nc.sbuf_tensor(name, shape, dt))

        def sem(name):
            return ctx.enter_context(nc.semaphore(name))

        x_sb = sb("x_sb", [P, NT, D])
        xn = sb("xn", [P, NT, D])
        zrow = sb("zrow", [P, NT, ROW])
        w_late = sb("w_late", [P, NT])
        row_late = sb("row_late", [P, NT], I32)
        z_now = sb("z_now", [P, 2, TB, D])
        xfT = sb("xfT", [P, 2, S])
        ident = sb("ident", [P, P])
        identb = sb("identb", [P, P], BF16)
        ones_b = sb("ones_b", [P, P], BF16)
        before = sb("before", [P, P], BF16)
        maskS = sb("maskS", [P, 3, G, 2 * QB], BF16)
        qmask = sb("qmask", [P, 4])
        vmask = sb("vmask", [P, 4, DH])
        zeros = sb("zeros", [P, 8, ROW])
        wA = sb("wA", [P, 4, D])
        wG = sb("wG", [P, E])
        w1_sb = sb("w1_sb", [P, E * DF])
        w2_sb = sb("w2_sb", [P, E * FC, D])
        cols = sb("cols", [P, 4])
        b_in = sb("b_in", [P, NBC])
        b_res = sb("b_res", [P, NBC])
        b_part = sb("b_part", [P, 3, NBC], BF16)
        b3 = sb("b3", [3, NB], BF16)
        st = sb("st", [P, NT, 6])
        mean = sb("mean", [P, 2, NT])
        rstd = sb("rstd", [P, 2, NT])
        lw = sb("lw", [P, 8, NT])
        r1 = {n: sb("s_" + n, [P, NT]) for n in ("m", "s", "rs", "p1", "k1", "p2", "k2", "den", "rd", "slf")}
        rev = sb("rev", [P, E])
        carry = sb("carry", [P, E, NT])
        thr = sb("thr", [P, NT])
        tile_no = sb("tile_no", [P, SLOT_TILES])
        ohb = sb("ohb", [P, E, NT], BF16)
        cnt = sb("cnt", [P, 2, E, NT])
        cum = sb("cum", [P, E, NT])
        base = sb("base", [P, E, NT])
        cmp = sb("cmp", [P, E, NT])
        ce = sb("ce", [P, E])
        ends = sb("ends", [P, E])
        starts = sb("starts", [P, E])
        emap = sb("emap", [P, SLOT_TILES, E])
        emap_f = sb("emap_f", [P, SLOT_TILES])
        emap_i = sb("emap_i", [P, SLOT_TILES], I32)
        slot = sb("slot", [P, 2, NT], I32)
        xnb = sb("xnb", [P, 2, TB, D])
        xnT = sb("xnT", [P, 2, S])
        qbd = sb("qbd", [P, NQ, 4, QB])
        kz = sb("kz", [P, G, QB + S])
        vaug = sb("vaug", [P, NQ, G, 2 * QB])
        negm = sb("negm", [P, 4, 8])
        pexp = sb("pexp", [P, 2, S])
        pT_all = sb("pT", [P, NQ + 1, 2 * G * QB])
        pT = pT_all[:, 0:NQ]
        flat_pT = pT_all[:].rearrange("p n c -> p (n c)")
        R = {n: flat_pT[:, NT * E * k:NT * E * (k + 1)].rearrange("p (t e) -> p t e", e=E)
             for k, n in enumerate(("lg", "d", "e", "p", "key", "oh1", "oh2", "pm"))}
        y_in = flat_pT[:, 0:4 * S].rearrange("p (u c t d) -> p u c t d", u=2, c=2, t=TB)
        rec = sb("rec", [P, 2, S])
        attnT = sb("attnT", [P, 2, S])
        xg = sb("xg", [P, RING, ROW])
        xgT = sb("xgT", [P, RING, P])
        h = sb("h", [P, 2, DF])
        hT = sb("hT", [P, 2, FC, P])
        y = sb("y", [P, RING, D])
        ps = ctx.enter_context(nc.psum_tensor("ps", [P, 8, 512], F32))

        x_in = [sem(f"x_in{n}") for n in range(4)]
        w_in = sem("w_in"); wG_in = sem("wG_in"); w1_in = sem("w1_in"); w2_in = sem("w2_in")
        b_got = sem("b_got"); b_put = sem("b_put"); b3_in = sem("b3_in"); b_done = sem("b_done")
        zero_put = sem("zero_put")
        pool = sem("pool")
        consts = sem("consts")
        dve = sem("dve")
        var_ready = sem("var_ready"); std_ready = sem("std_ready")
        xn_ready = sem("xn_ready")
        z_ready = sem("z_ready"); zT_ready = sem("zT_ready"); z_saved = sem("z_saved")
        xf_ready = sem("xf_ready"); gates_ready = sem("gates_ready")
        lg_d = sem("lg_d"); lg_e = sem("lg_e")
        oh_ready = sem("oh_ready"); counts_ready = sem("counts_ready")
        slots_ready = sem("slots_ready"); map_ready = sem("map_ready")
        sent = sem("sent")
        xnb_in = [sem(f"xnb_in{n}") for n in range(2)]; xnT_ps = sem("xnT_ps"); xnT_sb = sem("xnT_sb")
        q_ps = sem("q_ps"); k_ps = sem("k_ps"); q_sb = sem("q_sb"); k_sb = sem("k_sb")
        v_ps = sem("v_ps"); v_sb = sem("v_sb")
        s_ps = sem("s_ps"); m_sb = sem("m_sb"); p_sb = sem("p_sb"); pT_sb = sem("pT_sb")
        o_ps = sem("o_ps"); o_sb = sem("o_sb"); rec_sb = sem("rec_sb")
        a_ps = sem("a_ps"); a_sb = sem("a_sb")
        xg_in = [sem(f"xg_in{n}") for n in range(RING)]
        xgT_ps = sem("xgT_ps"); xgT_sb = sem("xgT_sb"); h_ps = sem("h_ps"); h_sb = sem("h_sb")
        hT_ps = sem("hT_ps"); hT_sb = sem("hT_sb"); y_ps = sem("y_ps"); y_sb = sem("y_sb"); y_going = sem("y_going")
        y_put = [sem(f"y_put{n}") for n in range(RING)]
        y_got = [sem(f"y_got{n}") for n in range(2)]
        y_sum = sem("y_sum"); out_put = [sem(f"out_put{n}") for n in range(2)]

        block = ctx.enter_context(nc.Block())
        XC = NT // 4
        x_tiles = x.rearrange("b (t p) d -> p (b t) d", p=P)
        out_tiles = out.rearrange("b (t p) d -> p (b t) d", p=P)
        xg_tiles = xg_dram.rearrange("(i p) c -> p i c", p=P)
        y_tiles = y_dram.rearrange("(c t p) d -> p c t d", c=2, p=P)

        def v_part(n, c):
            return ps[QB * n:QB * (n + 1), 2, :].rearrange("p (t g h d) -> p t g h d", t=TB, g=G, h=4)[:, :, :, c, :]

        def v_diag(n, c):
            return vaug[QB * c:QB * (c + 1)].rearrange("p (t n) g d -> p t n g d", n=4)[:, :, n, :, DH * c:DH * (c + 1)]

        @block.sync
        def _(sp):
            for n in range(4):
                sp.dma_start(x_sb[:, XC * n:XC * (n + 1), :], x_tiles[:, XC * n:XC * (n + 1), :]).then_inc(x_in[n], 16)
            sp.dma_start(b_in[:], bias_rows.rearrange("a (p c) -> (a p) c", p=P)).then_inc(b_got, 16)
            sp.dma_start(wG[:], w_gate).then_inc(wG_in, 16)
            sp.dma_start(cols[:], b_cols).then_inc(wG_in, 16)
            sp.dma_start(wA[:], w_attn).then_inc(w_in, 16)
            sp.dma_start(w1_sb[:], w1).then_inc(w1_in, 16)
            sp.dma_start(w2_sb[:], w2).then_inc(w2_in, 16)
            sp.wait_ge(b_done, 1)
            sp.dma_start(b3_dram.rearrange("a (p c) -> p a c", p=P), b_part[:]).then_inc(b_put, 16)
            sp.wait_ge(b_put, 16)
            sp.dma_start(b3[:], b3_dram).then_inc(b3_in, 16)
            sp.wait_ge(consts, 1)
            for n in range(SLOT_TILES // 8):
                sp.dma_start(xg_tiles[:, 8 * n:8 * (n + 1), :], zeros[:]).then_inc(zero_put, 16)
            with sp.Fori(0, B // 2) as i:
                for u in range(2):
                    sp.wait_ge(z_ready, 4 * (2 * i + u + 1))
                    sp.dma_start(zrow[:, bass.ds((2 * i + u) * TB, TB), 0:D], z_now[:, u]).then_inc(z_saved, 16)
            sp.wait_ge(xn_ready, NT)
            with sp.Fori(0, B // 2) as i:
                for u in range(2):
                    sp.wait_ge(xnT_ps, 2 * i + u) if u == 0 else sp.wait_ge(xnT_ps, 2 * i)
                    sp.dma_start(xnb[:, u], xn[:, bass.ds((2 * i + u) * TB, TB), :]).then_inc(xnb_in[u], 16)
            sp.wait_ge(sent, 16 * 2 * NT)
            for n in range(RING):
                sp.dma_start(xg[:, n, :], xg_tiles[:, n, :]).then_inc(xg_in[n], 16)
            with sp.Fori(0, SLOT_TILES // RING - 1) as i:
                for n in range(RING):
                    sp.wait_ge(y_put[n], 16 * (i + 1))
                    sp.dma_start(xg[:, n, :], xg_tiles[:, bass.ds(RING * (i + 1) + n, 1), :]).then_inc(xg_in[n], 16)
            for n in range(RING):
                sp.wait_ge(y_put[n], 16 * (SLOT_TILES // RING))
            with sp.Fori(0, B // 2) as i:
                for u in range(2):
                    sp.wait_ge(y_sum, 2 * i) if u == 0 else sp.wait_ge(y_sum, 2 * i)
                    for c in range(2):
                        sp.dma_start(y_in[:, u, c], y_tiles[:, c, bass.ds((2 * i + u) * TB, TB), :]).then_inc(y_got[u], 16)

        @block.gpsimd
        def _(gp):
            steps = [0]

            def step(ins):
                steps[0] += 1
                ins.then_inc(pool, 1)
                gp.wait_ge(pool, steps[0])

            step(nc.gpsimd.memset(ident[:], 0.0))
            step(nc.gpsimd.memset(before[:], 1.0))
            step(nc.gpsimd.memset(maskS[:], 0.0))
            step(nc.gpsimd.memset(qmask[:], float(DH) ** -0.5))
            step(nc.gpsimd.memset(vmask[:], 1.0))
            step(nc.gpsimd.memset(zeros[:], 0.0))
            step(nc.gpsimd.memset(carry[:], 1.0))
            step(nc.gpsimd.memset(kz[:], 0.0))
            step(nc.gpsimd.memset(ones_b[:], 1.0))
            step(nc.gpsimd.memset(vaug[:, :, :, 0:QB], 0.0))
            step(nc.gpsimd.iota(rev[:], [[-1, E]], base=E, channel_multiplier=0, allow_small_or_imprecise_dtypes=True))
            step(nc.gpsimd.iota(thr[:], [[P, NT]], base=0, channel_multiplier=0, allow_small_or_imprecise_dtypes=True))
            step(nc.gpsimd.iota(tile_no[:], [[1, SLOT_TILES]], base=0, channel_multiplier=0, allow_small_or_imprecise_dtypes=True))
            step(nc.gpsimd.iota(zrow[:, :, D + 1].bitcast(I32), [[P, NT]], base=0, channel_multiplier=1))
            step(nc.gpsimd.iota(row_late[:], [[P, NT]], base=TOKENS, channel_multiplier=1))
            step(nc.gpsimd.affine_select(out=ident[:], in_=ident[:], compare_op=ALU.not_equal, fill=1.0, base=0,
                             pattern=[[-1, P]], channel_multiplier=1))
            step(nc.gpsimd.affine_select(out=before[:], in_=before[:], compare_op=ALU.is_gt, fill=0.0, base=0,
                             pattern=[[1, P]], channel_multiplier=-1))
            step(nc.gpsimd.memset(carry[:, :, 0:1], 0.0))
            step(nc.gpsimd.iota(zeros[:, :, D + 1].bitcast(I32), [[0, 8]], base=2 * TOKENS, channel_multiplier=1))
            step(nc.gpsimd.affine_select(out=vmask[:], in_=vmask[:], compare_op=ALU.is_ge, fill=0.0, base=0,
                             pattern=[[-32, 4], [0, DH]], channel_multiplier=1))
            step(nc.gpsimd.affine_select(out=vmask[:], in_=vmask[:], compare_op=ALU.is_ge, fill=0.0, base=31,
                             pattern=[[32, 4], [0, DH]], channel_multiplier=-1))
            for j in range(4):
                part = slice(32 * j, 32 * j + 32)
                step(nc.gpsimd.affine_select(out=qmask[part, :], in_=qmask[part, :], compare_op=ALU.is_ge, fill=0.0, base=0,
                                 pattern=[[-DH, 4]], channel_multiplier=1))
                step(nc.gpsimd.affine_select(out=maskS[part], in_=maskS[part], compare_op=ALU.is_ge, fill=NEG, base=-1,
                                 pattern=[[0, 3 * G], [1, 2 * QB]], channel_multiplier=-1))
            for j in range(4):
                part = slice(32 * j, 32 * j + 32)
                step(nc.gpsimd.affine_select(out=qmask[part, :], in_=qmask[part, :], compare_op=ALU.is_ge, fill=0.0, base=DH - 1,
                                 pattern=[[DH, 4]], channel_multiplier=-1))
                step(nc.gpsimd.affine_select(out=maskS[part], in_=maskS[part], compare_op=ALU.is_ge, fill=NEG, base=QB,
                                 pattern=[[0, 3 * G], [-1, 2 * QB]], channel_multiplier=1))
            step(nc.gpsimd.tensor_copy(identb[:], ident[:]))
            step(nc.gpsimd.memset(maskS[:, 0, :, 0:QB], NEG))
            for u in range(1):
                step(nc.gpsimd.tensor_copy(vaug[:, :, :, QB:2 * QB],
                               vmask[:].rearrange("p h d -> p (h d)").unsqueeze(1).unsqueeze(1).to_broadcast([P, NQ, G, QB])
                               ))
            gp.sem_inc(consts, 1)
            gp.wait_ge(zero_put, 16 * (SLOT_TILES // 8))
            gp.wait_ge(z_saved, 16 * B)
            gp.wait_ge(slots_ready, 1)
            for c in range(2):
                if c == 1:
                    gp.wait_ge(sent, 16 * NT)
                    step(nc.gpsimd.tensor_copy(zrow[:, :, D], w_late[:]))
                    step(nc.gpsimd.tensor_copy(zrow[:, :, D + 1].bitcast(I32), row_late[:]))
                for t in range(NT):
                    gp.indirect_dma_start(xg_dram, bass.IndirectOffsetOnAxis(ap=slot[:, c, t:t + 1], axis=0),
                                          zrow[:, t, :], None).then_inc(sent, 16)
            last_row = gp.to_reg(2 * TOKENS - 1)
            with gp.Fori(0, SLOT_TILES // RING) as i:
                for n in range(RING):
                    gp.wait_ge(y_sb, RING * i + n + 1)
                    gp.sem_inc(y_going, 1)
                    gp.indirect_dma_start(y_dram, bass.IndirectOffsetOnAxis(ap=xg[:, n, D + 1:D + 2].bitcast(I32), axis=0),
                                          y[:, n, :], None, bounds_check=last_row, oob_is_err=False).then_inc(y_put[n], 16)

        @block.scalar
        def _(act):
            for n in range(2):
                act.wait_ge(var_ready, n + 1)
                nc.scalar.activation(lw[:, 6, :], lw[:, 5, :], ACT.Sqrt).then_inc(std_ready, 1)
            act.wait_ge(wG_in, 32)
            with act.Fori(0, B // 2) as i:
                for u in range(2):
                    act.wait_ge(zT_ready, 2 * i + u + 1)
                    if u == 0:
                        act.wait_ge(gates_ready, 2 * i)
                    nc.scalar.activation(xfT[:, u], ps[:, u, :], ACT.Identity, bias=cols[:, 3:4],
                                         scale=cols[:, 2:3]).then_inc(xf_ready, 1)
            act.wait_ge(lg_d, 1)
            nc.scalar.activation(R["e"], R["d"], ACT.Exp).then_inc(lg_e, 1)
            act.wait_ge(consts, 1)
            with act.Fori(0, B // 2) as i:
                for u in range(2):
                    b = 2 * i + u
                    act.wait_ge(xnT_ps, b + 1)
                    if u == 0:
                        act.wait_ge(a_ps, 2 * i)
                    nc.scalar.activation(xnT[:, u], ps[:, 0, :], ACT.Copy).then_inc(xnT_sb, 1)
                    act.wait_ge(k_ps, b + 1)
                    for g in range(G):
                        q = slice(32 * g, 32 * g + 32)
                        nc.scalar.activation(kz[q, g, QB:QB + S], ps[q, 1, :], ACT.Identity,
                                             bias=cols[q, 1:2]).then_inc(k_sb, 1)
                    act.wait_ge(v_ps, b + 1)
                    for n in (0, 1):
                        for c in range(4):
                            nc.scalar.activation(v_diag(n, c), v_part(n, c), ACT.Copy).then_inc(v_sb, 1)
                    for j in range(NQ // 2):
                        act.wait_ge(m_sb, b * (NQ // 2) + j + 1)
                        if j >= 2:
                            act.wait_ge(pT_sb, b * (NQ // 2) + j - 1)
                        for c in range(8):
                            nc.scalar.activation(pexp[:, j % 2, 64 * c:64 * c + 64], ps[:, 4 + j % 2, 64 * c:64 * c + 64],
                                                 ACT.Exp, bias=negm[:, j % 4, c:c + 1]).then_inc(p_sb, 1)
            act.wait_ge(a_sb, B)
            with act.Fori(0, SLOT_TILES // RING) as i:
                for n in range(RING):
                    k = RING * i + n
                    act.wait_ge(h_ps, k + 1)
                    if n >= 2:
                        act.wait_ge(hT_ps, k - 1)
                    else:
                        act.wait_ge(hT_ps, RING * i)
                    nc.scalar.activation(h[:, n % 2], ps[:, n % 2, :], ACT.Gelu).then_inc(h_sb, 1)
                    act.wait_ge(y_ps, k + 1)
                    if n == 0:
                        pass
                    act.wait_ge(y_put[n], 16 * i)
                    nc.scalar.activation(y[:, n, :], ps[:, 6 + n % 2, 0:D], ACT.Copy,
                                         scale=xg[:, n, D:D + 1]).then_inc(y_sb, 1)
            with act.Fori(0, B // 2) as i:
                for u in range(2):
                    b = 2 * i + u
                    act.wait_ge(y_sum, b + 1)
                    act.dma_start(out_tiles[:, bass.ds(b * TB, TB), :], x_sb[:, bass.ds(b * TB, TB), :]).then_inc(out_put[u], 16)
            for u in range(2):
                act.wait_ge(out_put[u], 16 * (B // 2))

        @block.vector
        def _(v):
            steps = [0]

            def link(ins):
                steps[0] += 1
                ins.then_inc(dve, 1)
                v.wait_ge(dve, steps[0])

            v.wait_ge(b_got, 16)
            link(nc.vector.tensor_copy(b_part[:, 0], b_in[:]))
            link(nc.vector.tensor_tensor(b_res[:], b_in[:], b_part[:, 0], ALU.subtract))
            link(nc.vector.tensor_copy(b_part[:, 1], b_res[:]))
            link(nc.vector.tensor_tensor(b_in[:], b_res[:], b_part[:, 1], ALU.subtract))
            nc.vector.tensor_copy(b_part[:, 2], b_in[:]).then_inc(b_done, 1)

            def statistics(n):
                me, mo, qe, qo = (st[:, :, k] for k in (1, 4, 2, 5))
                link(nc.vector.tensor_tensor(lw[:, 0], me, mo, ALU.subtract))
                link(nc.vector.tensor_tensor(lw[:, 1], me, mo, ALU.add))
                link(nc.vector.tensor_tensor(lw[:, 2], qe, qo, ALU.add))
                link(nc.vector.tensor_scalar(mean[:, n], lw[:, 1], 0.5, None, ALU.mult))
                link(nc.vector.tensor_tensor(lw[:, 3], lw[:, 0], lw[:, 0], ALU.mult))
                link(nc.vector.tensor_scalar(lw[:, 4], lw[:, 2], 1.0 / D, EPS_LN, ALU.mult, ALU.add))
                nc.vector.scalar_tensor_tensor(out=lw[:, 5], in0=lw[:, 3], scalar=0.25, in1=lw[:, 4],
                                               op0=ALU.mult, op1=ALU.add).then_inc(var_ready, 1)
                v.wait_ge(std_ready, n + 1)
                v.wait_ge(var_ready, n + 1)
                link(nc.vector.reciprocal(lw[:, 7], lw[:, 6]))
                link(nc.vector.tensor_tensor(lw[:, 0], lw[:, 7], lw[:, 7], ALU.mult))
                link(nc.vector.tensor_tensor(lw[:, 1], lw[:, 0], lw[:, 5], ALU.mult))
                link(nc.vector.tensor_scalar(lw[:, 2], lw[:, 1], -0.5, 1.5, ALU.mult, ALU.add))
                link(nc.vector.tensor_tensor(rstd[:, n], lw[:, 2], lw[:, 7], ALU.mult))

            for n in range(4):
                v.wait_ge(x_in[n], 16)
                with v.Fori(0, XC // 4) as i:
                    for u in range(4):
                        t = bass.ds(XC * n + 4 * i + u, 1)
                        ins = nc.vector.bn_stats(st[:, t, :].rearrange("p a s -> p (a s)"), x_sb[:, t, :].rearrange("p a s -> p (a s)"))
                    ins.then_inc(dve, 1)
            steps[0] += XC
            v.wait_ge(dve, steps[0])
            statistics(0)
            with v.Fori(0, NT // 4) as i:
                for u in range(4):
                    t = bass.ds(4 * i + u, 1)
                    nc.vector.tensor_scalar(xn[:, t, :], x_sb[:, t, :], mean[:, 0, t], rstd[:, 0, t],
                                            ALU.subtract, ALU.mult).then_inc(xn_ready, 1)
                for u in range(4):
                    t = bass.ds(4 * i + u, 1)
                    v.wait_ge(xn_ready, 4 * i + u + 1)
                    ins = nc.vector.bn_stats(st[:, t, :].rearrange("p a s -> p (a s)"), xn[:, t, :].rearrange("p a s -> p (a s)"))
                ins.then_inc(dve, 1)
            steps[0] += NT // 4
            v.wait_ge(dve, steps[0])
            statistics(1)
            with v.Fori(0, B // 2) as i:
                for u in range(2):
                    if u == 0:
                        v.wait_ge(zT_ready, 2 * i)
                        v.wait_ge(z_saved, 16 * (2 * i))
                    for j in range(TB):
                        t = bass.ds((2 * i + u) * TB + j, 1)
                        nc.vector.tensor_scalar(z_now[:, u, j, :], xn[:, t, :], mean[:, 1, t], rstd[:, 1, t],
                                                ALU.subtract, ALU.mult).then_inc(z_ready, 1)
            v.wait_ge(gates_ready, B)
            v.wait_ge(consts, 1)
            per_e = [P, NT, E]

            def bt(a):
                return a.unsqueeze(2).to_broadcast(per_e)

            rev_b = rev[:].unsqueeze(1).to_broadcast(per_e)
            link(nc.vector.tensor_copy(R["lg"], ps[:, 2, 0:NT * E].rearrange("p (t e) -> p t e", e=E)))
            link(nc.vector.tensor_reduce(r1["m"][:], R["lg"], AX.X, ALU.max))
            nc.vector.tensor_tensor(R["d"], R["lg"], bt(r1["m"][:]), ALU.subtract).then_inc(lg_d, 1)
            v.wait_ge(lg_e, 1)
            link(nc.vector.tensor_reduce(r1["s"][:], R["e"], AX.X, ALU.add))
            link(nc.vector.reciprocal(r1["rs"][:], r1["s"][:]))
            link(nc.vector.tensor_tensor(R["p"], R["e"], bt(r1["rs"][:]), ALU.mult))
            link(nc.vector.tensor_reduce(r1["p1"][:], R["p"], AX.X, ALU.max))
            link(nc.vector.tensor_tensor(R["key"], R["p"], bt(r1["p1"][:]), ALU.is_equal))
            link(nc.vector.tensor_tensor(R["key"], R["key"], rev_b, ALU.mult))
            link(nc.vector.tensor_reduce(r1["k1"][:], R["key"], AX.X, ALU.max))
            link(nc.vector.tensor_tensor(R["oh1"], rev_b, bt(r1["k1"][:]), ALU.is_equal))
            link(nc.vector.scalar_tensor_tensor(out=R["pm"], in0=R["oh1"], scalar=-2.0, in1=R["p"],
                                                op0=ALU.mult, op1=ALU.add))
            link(nc.vector.tensor_reduce(r1["p2"][:], R["pm"], AX.X, ALU.max))
            link(nc.vector.tensor_tensor(R["key"], R["pm"], bt(r1["p2"][:]), ALU.is_equal))
            link(nc.vector.tensor_tensor(R["key"], R["key"], rev_b, ALU.mult))
            link(nc.vector.tensor_reduce(r1["k2"][:], R["key"], AX.X, ALU.max))
            link(nc.vector.tensor_tensor(R["oh2"], rev_b, bt(r1["k2"][:]), ALU.is_equal))
            nc.vector.tensor_tensor(ohb[:].rearrange("p e t -> p t e"), R["oh1"], R["oh2"], ALU.add).then_inc(oh_ready, 1)
            link(nc.vector.scalar_tensor_tensor(out=r1["den"][:], in0=r1["p1"][:], scalar=EPS_TOPK, in1=r1["p2"][:],
                                                op0=ALU.add, op1=ALU.add))
            link(nc.vector.reciprocal(r1["rd"][:], r1["den"][:]))
            link(nc.vector.tensor_tensor(zrow[:, :, D], r1["p1"][:], r1["rd"][:], ALU.mult))
            link(nc.vector.tensor_tensor(w_late[:], r1["p2"][:], r1["rd"][:], ALU.mult))
            v.wait_ge(counts_ready, 1)
            link(nc.vector.tensor_copy(cnt[:], ps[:, 3, :].rearrange("p (a e t) -> p a e t", a=2, e=E)))
            flat = "p e t -> p (e t)"
            link(nc.vector.tensor_tensor_scan(cum[:].rearrange(flat), carry[:].rearrange(flat),
                                              cnt[:, 1].rearrange(flat), 0.0, ALU.mult, ALU.add))
            link(nc.vector.tensor_tensor(cmp[:], cum[:, :, NT - 1:NT].to_broadcast([P, E, NT]),
                                         thr[:].unsqueeze(1).to_broadcast([P, E, NT]), ALU.is_gt))
            link(nc.vector.tensor_reduce(ce[:], cmp[:], AX.X, ALU.add))
            link(nc.vector.tensor_tensor_scan(ends[:], ones_b[:, 0:E], ce[:], 0.0, ALU.mult, ALU.add))
            link(nc.vector.tensor_tensor(starts[:], ends[:], ce[:], ALU.subtract))
            link(nc.vector.tensor_tensor(base[:], cum[:], cnt[:, 1], ALU.subtract))
            link(nc.vector.tensor_tensor(base[:], base[:], cnt[:, 0], ALU.add))
            link(nc.vector.scalar_tensor_tensor(out=base[:], in0=starts[:].unsqueeze(2).to_broadcast([P, E, NT]),
                                                scalar=float(P), in1=base[:], op0=ALU.mult, op1=ALU.add))
            for c in range(2):
                link(nc.vector.tensor_tensor(R["key"], R[f"oh{c + 1}"], base[:].rearrange("p e t -> p t e"), ALU.mult))
                link(nc.vector.tensor_reduce(r1["slf"][:], R["key"], AX.X, ALU.add))
                link(nc.vector.tensor_copy(slot[:, c], r1["slf"][:]))
            v.sem_inc(slots_ready, 1)
            link(nc.vector.tensor_tensor(emap[:], tile_no[:].unsqueeze(2).to_broadcast([P, SLOT_TILES, E]),
                                         ends[:].unsqueeze(1).to_broadcast([P, SLOT_TILES, E]), ALU.is_ge))
            link(nc.vector.tensor_reduce(emap_f[:], emap[:], AX.X, ALU.add))
            nc.vector.tensor_scalar(emap_i[:], emap_f[:], float(E - 1), None, ALU.min).then_inc(map_ready, 1)
            link(nc.vector.tensor_tensor(x_sb[:], x_sb[:], xn[:], ALU.add))
            first = steps[0]

            with v.Fori(0, B // 2) as i:
                for u in range(2):
                    b = 2 * i + u
                    v.wait_ge(q_ps, b + 1)
                    for c in range(4):
                        nc.vector.tensor_scalar(qbd[:, :, c, :], ps[:, 0, :].rearrange("p (n q) -> p n q", q=QB), cols[:, 0:1], qmask[:, c:c + 1],
                                                ALU.add, ALU.mult).then_inc(q_sb, 1)
                    v.wait_ge(v_ps, b + 1)
                    for n in (2, 3):
                        for c in range(4):
                            nc.vector.tensor_copy(v_diag(n, c), v_part(n, c)).then_inc(v_sb, 1)
                    for j in range(NQ // 2 + 1):
                        if j < NQ // 2:
                            v.wait_ge(s_ps, b * (NQ // 2) + j + 1)
                            if j >= 4:
                                v.wait_ge(p_sb, 8 * (b * (NQ // 2) + j - 3))
                            nc.vector.tensor_reduce(negm[:, j % 4], ps[:, 4 + j % 2, :].rearrange("p (c k) -> p c k", k=2 * QB),
                                                    AX.X, ALU.max, negate=True).then_inc(m_sb, 1)
                        if j >= 1:
                            v.wait_ge(p_sb, 8 * (b * (NQ // 2) + j))
                            nc.vector.transpose(pT[:, 2 * (j - 1):2 * j, :].rearrange("p n c -> p (n c)"),
                                                pexp[:, (j - 1) % 2]).then_inc(pT_sb, 1)
                    v.wait_ge(o_ps, b + 1)
                    for k in range(2):
                        for half in range(2):
                            q = slice(64 * half + 32, 64 * half + 64)
                            nc.vector.reciprocal(rec[q, k, :], ps[q, 6 + k, :]).then_inc(rec_sb, 1)
                    for k in range(2):
                        for half in range(2):
                            v.wait_ge(rec_sb, 4 * b + 2 * k + half + 1)
                            g = 2 * k + half
                            nc.vector.tensor_tensor(attnT[32 * g:32 * g + 32, u, :], ps[64 * half:64 * half + 32, 6 + k, :],
                                                    rec[64 * half + 32:64 * half + 64, k, :], ALU.mult).then_inc(o_sb, 1)
                    v.wait_ge(a_ps, b + 1)
                    xs = x_sb[:, bass.ds(b * TB, TB), :]
                    nc.vector.tensor_tensor(xs, xs, ps[:, 1, :].rearrange("p (t d) -> p t d", t=TB), ALU.add).then_inc(a_sb, 1)
            with v.Fori(0, SLOT_TILES // RING) as i:
                for n in range(RING):
                    k = RING * i + n
                    if n == 0:
                        v.wait_ge(xgT_ps, k + 1)
                        nc.vector.tensor_scalar(xgT[:, 0], ps[:, 4, 0:P], cols[:, 2:3], cols[:, 3:4],
                                                ALU.mult, ALU.add).then_inc(xgT_sb, 1)
                    if n + 1 < RING:
                        v.wait_ge(xgT_ps, k + 2)
                        nc.vector.tensor_scalar(xgT[:, n + 1], ps[:, 4 + (n + 1) % 2, 0:P], cols[:, 2:3], cols[:, 3:4],
                                                ALU.mult, ALU.add).then_inc(xgT_sb, 1)
                    v.wait_ge(hT_ps, k + 1)
                    nc.vector.tensor_copy(hT[:, n % 2].rearrange("p c t -> p (c t)"), ps[:, 2 + n % 2, :]).then_inc(hT_sb, 1)
            with v.Fori(0, B // 2) as i:
                for u in range(2):
                    b = 2 * i + u
                    v.wait_ge(y_got[u], 32 * (i + 1))
                    xs = x_sb[:, bass.ds(b * TB, TB), :]
                    nc.vector.tensor_tensor(y_in[:, u, 0], y_in[:, u, 0], y_in[:, u, 1], ALU.add).then_inc(dve, 1)
                    v.wait_ge(dve, first + b + 1)
                    nc.vector.tensor_tensor(xs, xs, y_in[:, u, 0], ALU.add).then_inc(y_sum, 1)

        @block.tensor
        def _(pe):
            mm = nc.tensor.matmul

            def bias(dst, width, at, stop=False):
                return mm(dst, ones_b[0:3, :], b3[:, bass.ds(at, width)], start=True, stop=stop, skip_group_check=True)

            pe.wait_ge(consts, 1)
            pe.wait_ge(wG_in, 32)
            pe.wait_ge(b3_in, 16)
            with pe.Fori(0, B // 2) as i:
                for u in range(2):
                    b = 2 * i + u
                    if u == 0:
                        pe.wait_ge(xf_ready, 2 * i)
                    for j in range(TB):
                        pe.wait_ge(z_ready, b * TB + j + 1)
                        ins = nc.tensor.transpose(ps[:, u, P * j:P * (j + 1)], z_now[:, u, j, :], ident[:])
                    ins.then_inc(zT_ready, 1)
                for u in range(2):
                    b = 2 * i + u
                    pe.wait_ge(xf_ready, b + 1)
                    for j in range(TB):
                        dst = ps[:, 2, bass.ds((b * TB + j) * E, E)]
                        mm(dst, xfT[:, u, P * j:P * (j + 1)], wG[:], start=True, stop=False, skip_group_check=True)
                        ins = mm(dst, ones_b[0:3, :], b3[:, O_BG:O_BG + E], start=False, stop=True, skip_group_check=True)
                    ins.then_inc(gates_ready, 1)
            pe.wait_ge(oh_ready, 1)
            oh = ohb[:].rearrange("p e t -> p (e t)")
            mm(ps[:, 3, 0:E * NT], before[:], oh, start=True, stop=True)
            mm(ps[:, 3, E * NT:2 * E * NT], ones_b[:], oh, start=True, stop=True).then_inc(counts_ready, 1)
            pe.wait_ge(w_in, 16)
            pe.wait_ge(slots_ready, 1)
            with pe.Fori(0, B // 2) as i:
                for u in range(2):
                    b = 2 * i + u
                    pe.wait_ge(xnb_in[u], 16 * (i + 1))
                    pe.wait_ge(q_sb, 4 * b)
                    for j in range(TB):
                        ins = nc.tensor.transpose(ps[:, 0, P * j:P * (j + 1)], xnb[:, u, j, :], ident[:])
                    ins.then_inc(xnT_ps, 1)
                    pe.wait_ge(xnT_sb, b + 1)
                    pe.wait_ge(a_sb, b)
                    mm(ps[:, 1, :], wA[:, 1, :], xnT[:, u], start=True, stop=True).then_inc(k_ps, 1)
                    mm(ps[:, 0, :], wA[:, 0, :], xnT[:, u], start=True, stop=True).then_inc(q_ps, 1)
                    pe.wait_ge(v_sb, 16 * b)
                    mm(ps[:, 2, :], ones_b[0:3, :], b3[:, O_BV:O_BV + D].unsqueeze(1).to_broadcast([3, TB, D]),
                       start=True, stop=False, skip_group_check=True)
                    for j in range(TB):
                        ins = mm(ps[:, 2, D * j:D * (j + 1)], xnT[:, u, P * j:P * (j + 1)],
                                 wA[:, 2, :], start=False, stop=(j == TB - 1), skip_group_check=True)
                    ins.then_inc(v_ps, 1)
                    pe.wait_ge(k_sb, G * (b + 1))
                    pe.wait_ge(q_sb, 4 * (b + 1))

                    def values(m):
                        for g in range(G):
                            wide = 2 if m < NQ - 1 else 1
                            first_of_bank = m == 0 and g % 2 == 0
                            src = flat_pT
                            at = m * 2 * G * QB + g * 2 * QB + QB
                            step = 2 * G * QB - QB
                            if wide == 2:
                                a0 = src[:, at:at + 2 * step].rearrange("p (a c) -> p a c", a=2)[:, :, 0:QB]
                            else:
                                a0 = src[:, at:at + QB]
                            half = g % 2
                            ins = mm(ps[64 * half:64 * half + 64, 6 + g // 2, QB * m:QB * (m + wide)],
                                     vaug[:, m, g, :], a0, start=(m == 0), stop=(m == NQ - 1), skip_group_check=True)
                        return ins

                    for j in range(NQ // 2 + 2):
                        if j < NQ // 2:
                            k = b * (NQ // 2) + j
                            if j < 2:
                                pe.wait_ge(p_sb, 8 * b * (NQ // 2))
                            else:
                                pe.wait_ge(p_sb, 8 * (k - 1))
                            first_pair = 0 if j == 0 else 1
                            mm(ps[:, 4 + j % 2, :], identb[:], maskS[:, first_pair:first_pair + 2],
                               start=True, stop=False, skip_group_check=True)
                            for n in range(2):
                                blk = 2 * j + n
                                ins = mm(ps[:, 4 + j % 2, 256 * n:256 * (n + 1)], qbd[:, blk].rearrange("p h q -> p (h q)"),
                                         kz[:, :, QB * blk:QB * (blk + 2)], start=False, stop=(n == 1), skip_group_check=True)
                            ins.then_inc(s_ps, 1)
                        if j >= 2:
                            if j == 2:
                                pe.wait_ge(o_sb, 4 * b)
                                pe.wait_ge(v_sb, 16 * (b + 1))
                            pe.wait_ge(pT_sb, b * (NQ // 2) + j - 1)
                            if j > 2:
                                values(2 * (j - 2) - 1)
                            ins = values(2 * (j - 2))
                    values(NQ - 1).then_inc(o_ps, 1)
                    pe.wait_ge(o_sb, 4 * (b + 1))
                    for j in range(TB):
                        if j == 0:
                            mm(ps[:, 1, :], ones_b[0:3, :], b3[:, O_BO:O_BO + D].unsqueeze(1).to_broadcast([3, 4, D]),
                               start=True, stop=False, skip_group_check=True)
                        ins = mm(ps[:, 1, P * j:P * (j + 1)], attnT[:, u, P * j:P * (j + 1)], wA[:, 3, :],
                                 start=False, stop=(j == TB - 1), skip_group_check=True)
                    ins.then_inc(a_ps, 1)
            pe.wait_ge(w1_in, 16)
            pe.wait_ge(w2_in, 16)
            pe.wait_ge(map_ready, 1)
            pe.wait_ge(a_sb, B)

            def turn_rows(n, i):
                pe.wait_ge(xg_in[n], 16 * (i + 1))
                pe.wait_ge(xgT_sb, RING * i + (n - 1 if n >= 2 else 0))
                nc.tensor.transpose(ps[:, 4 + n % 2, 0:P], xg[:, n, 0:D], ident[:]).then_inc(xgT_ps, 1)

            with pe.Fori(0, SLOT_TILES // RING) as i:
                for n in range(RING + 1):
                    if n == 0:
                        turn_rows(0, i)
                    if n >= 1:
                        k = RING * i + n - 1
                        pe.wait_ge(h_sb, k + 1)
                        pe.wait_ge(hT_sb, RING * i + (n - 2 if n >= 3 else 0))
                        for c in range(FC):
                            ins = nc.tensor.transpose(ps[:, 2 + (n - 1) % 2, P * c:P * (c + 1)], h[:, (n - 1) % 2, P * c:P * (c + 1)], ident[:])
                        ins.then_inc(hT_ps, 1)
                    if n < RING:
                        if n + 1 < RING:
                            turn_rows(n + 1, i)
                        k = RING * i + n
                        e = pe.value_load(emap_i[0:1, bass.ds(k, 1)], min_val=0, max_val=E - 1)
                        pe.wait_ge(xgT_sb, k + 1)
                        pe.wait_ge(h_sb, RING * i + (n - 1 if n >= 2 else 0))
                        bias(ps[:, n % 2, :], DF, e * DF)
                        mm(ps[:, n % 2, :], xgT[:, n, :], w1_sb[:, bass.ds(e * DF, DF)], start=False, stop=True,
                           skip_group_check=True).then_inc(h_ps, 1)
                    if n >= 1:
                        k = RING * i + n - 1
                        pe.wait_ge(hT_sb, k + 1)
                        pe.wait_ge(y_sb, RING * i + (n - 2 if n >= 3 else 0))
                        bias(ps[:, 6 + (n - 1) % 2, 0:D], D, e_before * D + O_B2)
                        for c in range(FC):
                            ins = mm(ps[:, 6 + (n - 1) % 2, 0:D], hT[:, (n - 1) % 2, c, :],
                                     w2_sb[:, bass.ds(e_before * FC + c, 1), :], start=False, stop=(c == FC - 1), skip_group_check=True)
                        ins.then_inc(y_ps, 1)
                    e_before = e


def kernel(**inputs):
    import numpy as np
    import concourse.bacc as bacc
    from concourse.bass_utils import run_bass_kernel_spmd

    a = {k[3:]: np.asarray(v) for k, v in inputs.items()}
    E, DF, D = a["ffn_W1"].shape
    w_attn = np.stack([a["attn_W" + n].T for n in "qkvo"], axis=1)
    b_cols = np.stack([a["attn_bq"], a["attn_bk"], a["ffn_gamma"], a["ffn_beta"]], axis=1)
    rows = np.concatenate([a["ffn_b1"].ravel(), a["ffn_b2"].ravel(), a["attn_bo"], a["attn_bv"], a["ffn_bg"]])
    width = -(-rows.size // 128) * 128
    bias_rows = np.zeros((1, width), rows.dtype)
    bias_rows[0, :rows.size] = rows
    w1 = a["ffn_W1"].transpose(2, 0, 1).reshape(D, E * DF)
    w2 = a["ffn_W2"].transpose(2, 0, 1).reshape(DF // 128, 128, E, D).transpose(1, 2, 0, 3).reshape(128, E * (DF // 128), D)
    ins = {"x": a["attn_x"], "w_attn": w_attn, "b_cols": b_cols, "bias_rows": bias_rows,
           "w_gate": a["ffn_Wg"].T, "w1": w1, "w2": w2}
    ins = {k: np.ascontiguousarray(v) for k, v in ins.items()}

    nc = bacc.Bacc("TRN2", target_bir_lowering=False, num_devices=1)
    args = [nc.dram_tensor("in_" + k, v.shape, F32, kind="ExternalInput").ap() for k, v in ins.items()]
    out = nc.dram_tensor("out", a["attn_x"].shape, F32, kind="ExternalOutput").ap()
    attention_and_experts(nc, *args, out)
    got = run_bass_kernel_spmd(nc, [{"in_" + k: v for k, v in ins.items()}], core_ids=[0])
    return got.results[0]["out"]
```

```python
from contextlib import ExitStack

import concourse.bass as bass
from concourse import mybir

F32 = mybir.dt.float32
BF16 = mybir.dt.bfloat16
I32 = mybir.dt.int32
ALU = mybir.AluOpType
ACT = mybir.ActivationFunctionType
AX = mybir.AxisListType

P = 128
NEG = -1.0e30
EPS_LN = 1e-5
EPS_TOPK = 1e-8


def attention_and_experts(nc, x, w_attn, b_cols, bias_rows, w_gate, w1, w2, out):
    B, S, D = x.shape
    TB = S // P
    NT = B * TB
    TOKENS = NT * P
    E = w_gate.shape[1]
    DF = w1.shape[2] * P // (P + 1)
    FC = DF // P
    W1C = DF + FC
    DH = 8
    QB = 32
    NQ = S // QB
    G = 4
    SLOT_TILES = 2 * NT + E
    SLOTS = SLOT_TILES * P
    MAPPED = SLOT_TILES + 8
    ROW = D + 2
    RING = 8
    SR = 4
    TURN_LAG, WEIGH_LAG = 2, 3
    YRING = 4
    NB = bias_rows.shape[1]
    O_B2, O_BO, O_BV, O_BG = 0, E * D, E * D + D, E * D + 2 * D
    NBC = NB // P

    xg_dram = nc.dram_tensor("slot_rows", (SLOTS, ROW), F32, kind="Internal").ap()
    y_dram = nc.dram_tensor("expert_rows", (2 * TOKENS, D), F32, kind="Internal").ap()
    b3_dram = nc.dram_tensor("bias_parts", (3, NB), BF16, kind="Internal").ap()

    with ExitStack() as ctx:
        def sb(name, shape, dt=F32):
            return ctx.enter_context(nc.sbuf_tensor(name, shape, dt))

        def sem(name):
            return ctx.enter_context(nc.semaphore(name))

        x_sb = sb("x_sb", [P, NT, D])
        xn = sb("xn", [P, NT, D])
        zrow = sb("zrow", [P, NT, ROW])
        w_late = sb("w_late", [P, NT])
        row_late = sb("row_late", [P, NT], I32)
        ident = sb("ident", [P, P])
        identb = sb("identb", [P, P], BF16)
        ones_b = sb("ones_b", [P, P], BF16)
        before = sb("before", [P, P], BF16)
        maskS = sb("maskS", [P, 3, G, 2 * QB], BF16)
        qmask = sb("qmask", [P, 4])
        vmask = sb("vmask", [P, 4, DH])
        zeros = sb("zeros", [P, 8, ROW])
        wA = sb("wA", [P, 4, D])
        wG = sb("wG", [P, E])
        w1_sb = sb("w1_sb", [P, E, W1C])
        w2_sb = sb("w2_sb", [P, E * FC, D])
        cols = sb("cols", [P, 4])
        b_in = sb("b_in", [P, NBC])
        b_res = sb("b_res", [P, NBC])
        b_part = sb("b_part", [P, 3, NBC], BF16)
        b3 = sb("b3", [3, NB], BF16)
        st = sb("st", [P, NT, 6])
        mean = sb("mean", [P, 2, NT])
        rstd = sb("rstd", [P, 2, NT])
        lw = sb("lw", [P, 8, NT])
        r1 = {n: sb("s_" + n, [P, NT]) for n in ("m", "s", "rs", "p1", "k1", "p2", "k2", "den", "rd", "slf")}
        rev = sb("rev", [P, E])
        carry = sb("carry", [P, E, NT])
        thr = sb("thr", [P, NT])
        tile_no = sb("tile_no", [P, MAPPED])
        ohb = sb("ohb", [P, E, NT], BF16)
        cnt = sb("cnt", [P, 2, E, NT])
        cum = sb("cum", [P, E, NT])
        base = sb("base", [P, E, NT])
        cmp = sb("cmp", [P, E, NT])
        ce = sb("ce", [P, E])
        ends = sb("ends", [P, E])
        starts = sb("starts", [P, E])
        emap = sb("emap", [P, MAPPED, E])
        emap_f = sb("emap_f", [P, MAPPED])
        emap_i = sb("emap_i", [P, MAPPED], I32)
        slot = sb("slot", [P, 2, NT], I32)
        xnb = sb("xnb", [P, TB, D])
        xnT = sb("xnT", [P, S])
        qbd = sb("qbd", [P, 2, NQ, 4, QB])
        kz = sb("kz", [P, 2, G, QB + S])
        vbd = sb("vbd", [P, 2, NQ, G, 4 * DH])
        negm = sb("negm", [P, SR, 8])
        pexp = sb("pexp", [P, SR, S])
        pT_all = sb("pT", [P, NQ + 1, 2 * G * QB])
        pT = pT_all[:, 0:NQ]
        rec = sb("rec", [P, S])
        o_now = sb("o_now", [P, S])
        attnT = sb("attnT", [P, S])
        flat_pT = pT_all[:].rearrange("p n c -> p (n c)")
        R = {n: flat_pT[:, NT * E * k:NT * E * (k + 1)].rearrange("p (t e) -> p t e", e=E)
             for k, n in enumerate(("lg", "d", "e", "p", "key", "oh1", "oh2", "pm"))}
        y_in = flat_pT[:, 0:4 * S].rearrange("p (u c t d) -> p u c t d", u=2, c=2, t=TB)
        z_now = qbd[:, 1, 0:NQ // 2].rearrange("p n h q -> p (n h q)").rearrange("p (u t d) -> p u t d", u=2, t=TB)
        xfT = qbd[:, 1, NQ // 2:NQ].rearrange("p n h q -> p (n h q)").rearrange("p (u s) -> p u s", u=2)
        xg = sb("xg", [P, RING, ROW])
        flat_kz = kz[:].rearrange("p u g k -> p (u g k)")
        O_W, O_X, O_Y = 2 * DF, 2 * DF + 2 * W1C, 2 * DF + 2 * W1C + 2 * P
        hT = flat_kz[:, 0:O_W].rearrange("p (u c t) -> p u c t", u=2, c=FC)
        w1_now = flat_kz[:, O_W:O_X].rearrange("p (u f) -> p u f", u=2)
        xgT = flat_kz[:, O_X:O_Y].rearrange("p (u t) -> p u t", u=2)
        y = flat_kz[:, O_Y:O_Y + YRING * D].rearrange("p (u d) -> p u d", u=YRING)
        ps = ctx.enter_context(nc.psum_tensor("ps", [P, 8, 512], F32))

        x_in = [sem(f"x_in{n}") for n in range(4)]
        w_in = sem("w_in"); wG_in = sem("wG_in"); w1_in = sem("w1_in"); w2_in = sem("w2_in")
        b_got = sem("b_got"); b_put = sem("b_put"); b3_in = sem("b3_in"); b_done = sem("b_done")
        zero_put = sem("zero_put")
        pool = sem("pool")
        consts = sem("consts")
        dve = sem("dve")
        var_ready = sem("var_ready"); std_ready = sem("std_ready")
        xn_ready = sem("xn_ready")
        z_ready = sem("z_ready"); zT_ready = sem("zT_ready"); z_saved = sem("z_saved")
        xf_ready = sem("xf_ready"); gates_ready = sem("gates_ready")
        lg_d = sem("lg_d"); lg_e = sem("lg_e")
        oh_ready = sem("oh_ready"); counts_ready = sem("counts_ready")
        slots_ready = sem("slots_ready"); map_ready = sem("map_ready")
        sent = sem("sent")
        xnb_in = sem("xnb_in"); xnT_ps = sem("xnT_ps"); xnT_sb = sem("xnT_sb")
        q_ps = sem("q_ps"); k_ps = sem("k_ps"); q_sb = sem("q_sb"); k_sb = sem("k_sb")
        v_ps = sem("v_ps"); v_sb = sem("v_sb")
        s_ps = sem("s_ps"); m_sb = sem("m_sb"); p_sb = sem("p_sb"); pT_sb = sem("pT_sb")
        o_ps = sem("o_ps"); o_out = sem("o_out"); o_sb = sem("o_sb"); rec_sb = sem("rec_sb")
        a_ps = sem("a_ps"); a_sb = sem("a_sb")
        xg_in = [sem(f"xg_in{n}") for n in range(RING)]
        xgT_ps = sem("xgT_ps"); xgT_sb = sem("xgT_sb"); w1_set = sem("w1_set")
        hT_ps = sem("hT_ps"); hT_sb = sem("hT_sb"); y_ps = sem("y_ps"); y_sb = sem("y_sb"); y_going = sem("y_going")
        y_put = [sem(f"y_put{n}") for n in range(RING)]
        y_got = [sem(f"y_got{n}") for n in range(2)]
        y_sum = sem("y_sum"); out_put = [sem(f"out_put{n}") for n in range(2)]

        block = ctx.enter_context(nc.Block())
        XC = NT // 4
        x_tiles = x.rearrange("b (t p) d -> p (b t) d", p=P)
        out_tiles = out.rearrange("b (t p) d -> p (b t) d", p=P)
        xg_tiles = xg_dram.rearrange("(i p) c -> p i c", p=P)
        y_tiles = y_dram.rearrange("(c t p) d -> p c t d", c=2, p=P)

        PAIRS = NQ // 2
        PE_XN, PE_V, PE_K, PE_Q, PE_OUT = 0, 2, 4, 5, 6
        ACT_XN, ACT_V, ACT_K, ACT_O = 0, (2, 2), (4, 5), 2
        DVE_Q, DVE_INVERT, DVE_NORMALISE, DVE_ADD = (5, 5), (2, 4), 4, 6
        MAXIMA_FIRST = False
        LOOPED = (B - 2) // 2
        FIRST = RING - 1
        TURNS = (SLOT_TILES - 1 - FIRST) // RING

        def wait(engine, semaphore, count):
            if not isinstance(count, int) or count > 0:
                engine.wait_ge(semaphore, count)

        def run_experts(engine, step):
            for r in range(FIRST):
                step(0, r)
            with engine.Fori(0, TURNS) as i:
                for r in range(FIRST, FIRST + RING):
                    step(i + r // RING, r % RING)
            for k in range(SLOT_TILES - 1, SLOT_TILES + 1):
                step(k // RING, k % RING)

        def v_part(n, c):
            return ps[QB * n:QB * (n + 1), 0, :].rearrange("p (t g h d) -> p t g h d", t=TB, g=G, h=4)[:, :, :, c, :]

        def v_diag(u, n, c):
            return vbd[QB * c:QB * (c + 1), u].rearrange("p (t n) g d -> p t n g d", n=4)[:, :, n, :, DH * c:DH * (c + 1)]

        @block.sync
        def _(sp):
            for n in range(4):
                sp.dma_start(x_sb[:, XC * n:XC * (n + 1), :], x_tiles[:, XC * n:XC * (n + 1), :]).then_inc(x_in[n], 16)
            sp.dma_start(b_in[:], bias_rows.rearrange("a (p c) -> (a p) c", p=P)).then_inc(b_got, 16)
            sp.dma_start(wG[:], w_gate).then_inc(wG_in, 16)
            sp.dma_start(cols[:], b_cols).then_inc(wG_in, 16)
            sp.dma_start(wA[:], w_attn).then_inc(w_in, 16)
            sp.dma_start(w1_sb[:], w1).then_inc(w1_in, 16)
            sp.dma_start(w2_sb[:], w2).then_inc(w2_in, 16)
            sp.wait_ge(b_done, 1)
            sp.dma_start(b3_dram.rearrange("a (p c) -> p a c", p=P), b_part[:]).then_inc(b_put, 16)
            sp.wait_ge(b_put, 16)
            sp.dma_start(b3[:], b3_dram).then_inc(b3_in, 16)
            sp.wait_ge(consts, 1)
            for n in range(SLOT_TILES // 8):
                sp.dma_start(xg_tiles[:, 8 * n:8 * (n + 1), :], zeros[:]).then_inc(zero_put, 16)
            with sp.Fori(0, B // 2) as i:
                for u in range(2):
                    sp.wait_ge(z_ready, 4 * (2 * i + u + 1))
                    sp.dma_start(zrow[:, bass.ds((2 * i + u) * TB, TB), 0:D], z_now[:, u]).then_inc(z_saved, 16)
            sp.wait_ge(xn_ready, NT)
            sp.dma_start(xnb[:], xn[:, 0:TB, :]).then_inc(xnb_in, 16)
            with sp.Fori(1, B) as b:
                sp.wait_ge(xnT_ps, b)
                sp.dma_start(xnb[:], xn[:, bass.ds(b * TB, TB), :]).then_inc(xnb_in, 16)
            sp.wait_ge(sent, 16 * 2 * NT)
            for n in range(RING):
                sp.dma_start(xg[:, n, :], xg_tiles[:, n, :]).then_inc(xg_in[n], 16)
            with sp.Fori(1, SLOT_TILES // RING) as i:
                for n in range(RING):
                    sp.wait_ge(y_put[n], 16 * i)
                    sp.dma_start(xg[:, n, :], xg_tiles[:, bass.ds(RING * i + n, 1), :]).then_inc(xg_in[n], 16)
            for n in range(RING):
                sp.wait_ge(y_put[n], 16 * (SLOT_TILES // RING))
            for u in range(2):
                for c in range(2):
                    sp.dma_start(y_in[:, u, c], y_tiles[:, c, TB * u:TB * (u + 1), :]).then_inc(y_got[u], 16)
            with sp.Fori(1, B // 2) as i:
                for u in range(2):
                    sp.wait_ge(y_sum, 2 * i + u - 1)
                    for c in range(2):
                        sp.dma_start(y_in[:, u, c], y_tiles[:, c, bass.ds((2 * i + u) * TB, TB), :]).then_inc(y_got[u], 16)

        @block.gpsimd
        def _(gp):
            steps = [0]

            def step(ins):
                steps[0] += 1
                ins.then_inc(pool, 1)
                gp.wait_ge(pool, steps[0])

            step(nc.gpsimd.memset(ident[:], 0.0))
            step(nc.gpsimd.memset(before[:], 1.0))
            step(nc.gpsimd.memset(maskS[:], 0.0))
            step(nc.gpsimd.memset(qmask[:], float(DH) ** -0.5))
            step(nc.gpsimd.memset(vmask[:], 1.0))
            step(nc.gpsimd.memset(zeros[:], 0.0))
            step(nc.gpsimd.memset(carry[:], 1.0))
            step(nc.gpsimd.memset(kz[:], 0.0))
            step(nc.gpsimd.memset(ones_b[:], 1.0))
            step(nc.gpsimd.memset(vbd[:], 0.0))
            step(nc.gpsimd.iota(rev[:], [[-1, E]], base=E, channel_multiplier=0, allow_small_or_imprecise_dtypes=True))
            step(nc.gpsimd.iota(thr[:], [[P, NT]], base=0, channel_multiplier=0, allow_small_or_imprecise_dtypes=True))
            step(nc.gpsimd.iota(tile_no[:], [[1, MAPPED]], base=0, channel_multiplier=0, allow_small_or_imprecise_dtypes=True))
            step(nc.gpsimd.iota(zrow[:, :, D + 1].bitcast(I32), [[P, NT]], base=0, channel_multiplier=1))
            step(nc.gpsimd.iota(row_late[:], [[P, NT]], base=TOKENS, channel_multiplier=1))
            step(nc.gpsimd.affine_select(out=ident[:], in_=ident[:], compare_op=ALU.not_equal, fill=1.0, base=0,
                             pattern=[[-1, P]], channel_multiplier=1))
            step(nc.gpsimd.affine_select(out=before[:], in_=before[:], compare_op=ALU.is_gt, fill=0.0, base=0,
                             pattern=[[1, P]], channel_multiplier=-1))
            step(nc.gpsimd.memset(carry[:, :, 0:1], 0.0))
            step(nc.gpsimd.iota(zeros[:, :, D + 1].bitcast(I32), [[0, 8]], base=2 * TOKENS, channel_multiplier=1))
            step(nc.gpsimd.affine_select(out=vmask[:], in_=vmask[:], compare_op=ALU.is_ge, fill=0.0, base=0,
                             pattern=[[-32, 4], [0, DH]], channel_multiplier=1))
            step(nc.gpsimd.affine_select(out=vmask[:], in_=vmask[:], compare_op=ALU.is_ge, fill=0.0, base=31,
                             pattern=[[32, 4], [0, DH]], channel_multiplier=-1))
            for j in range(4):
                part = slice(32 * j, 32 * j + 32)
                step(nc.gpsimd.affine_select(out=qmask[part, :], in_=qmask[part, :], compare_op=ALU.is_ge, fill=0.0, base=0,
                                 pattern=[[-DH, 4]], channel_multiplier=1))
                step(nc.gpsimd.affine_select(out=maskS[part], in_=maskS[part], compare_op=ALU.is_ge, fill=NEG, base=-1,
                                 pattern=[[0, 3 * G], [1, 2 * QB]], channel_multiplier=-1))
            for j in range(4):
                part = slice(32 * j, 32 * j + 32)
                step(nc.gpsimd.affine_select(out=qmask[part, :], in_=qmask[part, :], compare_op=ALU.is_ge, fill=0.0, base=DH - 1,
                                 pattern=[[DH, 4]], channel_multiplier=-1))
                step(nc.gpsimd.affine_select(out=maskS[part], in_=maskS[part], compare_op=ALU.is_ge, fill=NEG, base=QB,
                                 pattern=[[0, 3 * G], [-1, 2 * QB]], channel_multiplier=1))
            step(nc.gpsimd.tensor_copy(identb[:], ident[:]))
            step(nc.gpsimd.memset(maskS[:, 0, :, 0:QB], NEG))
            gp.sem_inc(consts, 1)
            gp.wait_ge(zero_put, 16 * (SLOT_TILES // 8))
            gp.wait_ge(z_saved, 16 * B)
            gp.wait_ge(slots_ready, 1)
            for c in range(2):
                if c == 1:
                    gp.wait_ge(sent, 16 * NT)
                    step(nc.gpsimd.tensor_copy(zrow[:, :, D], w_late[:]))
                    step(nc.gpsimd.tensor_copy(zrow[:, :, D + 1].bitcast(I32), row_late[:]))
                for t in range(NT):
                    gp.indirect_dma_start(xg_dram, bass.IndirectOffsetOnAxis(ap=slot[:, c, t:t + 1], axis=0),
                                          zrow[:, t, :], None).then_inc(sent, 16)
            last_row = gp.to_reg(2 * TOKENS - 1)
            with gp.Fori(0, SLOT_TILES // RING) as i:
                for n in range(RING):
                    gp.wait_ge(y_sb, RING * i + n + 1)
                    gp.sem_inc(y_going, 1)
                    gp.indirect_dma_start(y_dram, bass.IndirectOffsetOnAxis(ap=xg[:, n, D + 1:D + 2].bitcast(I32), axis=0),
                                          y[:, n % YRING, :], None, bounds_check=last_row, oob_is_err=False).then_inc(y_put[n], 16)

        @block.scalar
        def _(act):
            for n in range(2):
                act.wait_ge(var_ready, n + 1)
                nc.scalar.activation(lw[:, 6, :], lw[:, 5, :], ACT.Sqrt).then_inc(std_ready, 1)
            act.wait_ge(wG_in, 32)

            def two_xf(i):
                for u in range(2):
                    act.wait_ge(zT_ready, 2 * i + u + 1)
                    wait(act, gates_ready, 2 * i + u - 1)
                    nc.scalar.activation(xfT[:, u], ps[:, u, :], ACT.Identity, bias=cols[:, 3:4],
                                         scale=cols[:, 2:3]).then_inc(xf_ready, 1)

            two_xf(0)
            with act.Fori(1, B // 2) as i:
                two_xf(i)
            act.wait_ge(lg_d, 1)
            nc.scalar.activation(R["e"], R["d"], ACT.Exp).then_inc(lg_e, 1)
            act.wait_ge(consts, 1)

            def turned_xn(b):
                act.wait_ge(xnT_ps, b + 1)
                nc.scalar.activation(xnT[:], ps[:, 0, :], ACT.Copy).then_inc(xnT_sb, 1)

            def keys(b, u, groups=range(G)):
                act.wait_ge(k_ps, b + 1)
                for g in groups:
                    q = slice(32 * g, 32 * g + 32)
                    nc.scalar.activation(kz[q, u, g, QB:QB + S], ps[q, 1, :], ACT.Identity,
                                         bias=cols[q, 1:2]).then_inc(k_sb, 1)

            def values(b, u, quadrants=range(4)):
                act.wait_ge(v_ps, b + 1)
                for n in quadrants:
                    for c in range(4):
                        nc.scalar.activation(v_diag(u, n, c), v_part(n, c), ACT.Copy).then_inc(v_sb, 1)

            def exponentials(b, j):
                k = b * PAIRS + j
                act.wait_ge(m_sb, k + 1)
                wait(act, pT_sb, k + 1 - SR)
                for c in range(8):
                    nc.scalar.activation(pexp[:, j % SR, 64 * c:64 * c + 64], ps[:, 2 + j % SR, 64 * c:64 * c + 64],
                                         ACT.Exp, bias=negm[:, j % SR, c:c + 1]).then_inc(p_sb, 1)

            def values_out(b):
                act.wait_ge(o_ps, b + 1)
                nc.scalar.activation(o_now[:], ps[:, 6, :], ACT.Copy).then_inc(o_out, 1)

            def sequence(b, u, first, last):
                for j in range(PAIRS):
                    exponentials(b, j)
                    if j == ACT_O and not first:
                        values_out(b - 1)
                    if last:
                        continue
                    if j == ACT_XN:
                        turned_xn(b + 1)
                    for part in range(2):
                        if j == ACT_V[part]:
                            values(b + 1, 1 - u, (2 * part, 2 * part + 1))
                        if j == ACT_K[part]:
                            keys(b + 1, 1 - u, (2 * part, 2 * part + 1))

            turned_xn(0)
            values(0, 0)
            keys(0, 0)
            sequence(0, 0, True, False)
            with act.Fori(0, LOOPED) as i:
                for u in range(2):
                    sequence(1 + 2 * i + u, 1 - u, False, False)
            sequence(B - 1, 1, False, True)
            values_out(B - 1)
            act.wait_ge(s_ps, B * PAIRS)

            def expert_step(turn, r):
                k = RING * turn + r
                last = isinstance(k, int) and k == SLOT_TILES
                if not last:
                    act.wait_ge(hT_ps, k + 1)
                    wait(act, y_ps, k - 1)
                    for c in range(FC):
                        nc.scalar.activation(hT[:, r % 2, c], ps[:, r % 2, P * c:P * (c + 1)], ACT.Gelu,
                                             bias=w1_now[:, r % 2, DF + c:DF + c + 1]).then_inc(hT_sb, 1)
                if isinstance(k, int) and k == 0:
                    return
                before = (r - 1) % RING
                act.wait_ge(y_ps, k)
                wait(act, y_put[(r - 1 - YRING) % RING], 16 * (turn + (r - 1 - YRING) // RING + 1))
                nc.scalar.activation(y[:, before % YRING, :], ps[:, 6 + before % 2, 0:D], ACT.Copy,
                                     scale=xg[:, before, D:D + 1]).then_inc(y_sb, 1)

            run_experts(act, expert_step)
            with act.Fori(0, B // 2) as i:
                for u in range(2):
                    b = 2 * i + u
                    act.wait_ge(y_sum, b + 1)
                    act.dma_start(out_tiles[:, bass.ds(b * TB, TB), :], x_sb[:, bass.ds(b * TB, TB), :]).then_inc(out_put[u], 16)
            for u in range(2):
                act.wait_ge(out_put[u], 16 * (B // 2))

        @block.vector
        def _(v):
            steps = [0]

            def link(ins):
                steps[0] += 1
                ins.then_inc(dve, 1)
                v.wait_ge(dve, steps[0])

            v.wait_ge(b_got, 16)
            link(nc.vector.tensor_copy(b_part[:, 0], b_in[:]))
            link(nc.vector.tensor_tensor(b_res[:], b_in[:], b_part[:, 0], ALU.subtract))
            link(nc.vector.tensor_copy(b_part[:, 1], b_res[:]))
            link(nc.vector.tensor_tensor(b_in[:], b_res[:], b_part[:, 1], ALU.subtract))
            nc.vector.tensor_copy(b_part[:, 2], b_in[:]).then_inc(b_done, 1)

            def statistics(n):
                me, mo, qe, qo = (st[:, :, k] for k in (1, 4, 2, 5))
                link(nc.vector.tensor_tensor(lw[:, 0], me, mo, ALU.subtract))
                link(nc.vector.tensor_tensor(lw[:, 1], me, mo, ALU.add))
                link(nc.vector.tensor_tensor(lw[:, 2], qe, qo, ALU.add))
                link(nc.vector.tensor_scalar(mean[:, n], lw[:, 1], 0.5, None, ALU.mult))
                link(nc.vector.tensor_tensor(lw[:, 3], lw[:, 0], lw[:, 0], ALU.mult))
                link(nc.vector.tensor_scalar(lw[:, 4], lw[:, 2], 1.0 / D, EPS_LN, ALU.mult, ALU.add))
                nc.vector.scalar_tensor_tensor(out=lw[:, 5], in0=lw[:, 3], scalar=0.25, in1=lw[:, 4],
                                               op0=ALU.mult, op1=ALU.add).then_inc(var_ready, 1)
                v.wait_ge(std_ready, n + 1)
                v.wait_ge(var_ready, n + 1)
                link(nc.vector.reciprocal(lw[:, 7], lw[:, 6]))
                link(nc.vector.tensor_tensor(lw[:, 0], lw[:, 7], lw[:, 7], ALU.mult))
                link(nc.vector.tensor_tensor(lw[:, 1], lw[:, 0], lw[:, 5], ALU.mult))
                link(nc.vector.tensor_scalar(lw[:, 2], lw[:, 1], -0.5, 1.5, ALU.mult, ALU.add))
                link(nc.vector.tensor_tensor(rstd[:, n], lw[:, 2], lw[:, 7], ALU.mult))

            for n in range(4):
                v.wait_ge(x_in[n], 16)
                with v.Fori(0, XC // 4) as i:
                    for u in range(4):
                        t = bass.ds(XC * n + 4 * i + u, 1)
                        ins = nc.vector.bn_stats(st[:, t, :].rearrange("p a s -> p (a s)"), x_sb[:, t, :].rearrange("p a s -> p (a s)"))
                    ins.then_inc(dve, 1)
            steps[0] += XC
            v.wait_ge(dve, steps[0])
            statistics(0)
            with v.Fori(0, NT // 4) as i:
                for u in range(4):
                    t = bass.ds(4 * i + u, 1)
                    nc.vector.tensor_scalar(xn[:, t, :], x_sb[:, t, :], mean[:, 0, t], rstd[:, 0, t],
                                            ALU.subtract, ALU.mult).then_inc(xn_ready, 1)
                for u in range(4):
                    t = bass.ds(4 * i + u, 1)
                    v.wait_ge(xn_ready, 4 * i + u + 1)
                    ins = nc.vector.bn_stats(st[:, t, :].rearrange("p a s -> p (a s)"), xn[:, t, :].rearrange("p a s -> p (a s)"))
                ins.then_inc(dve, 1)
            steps[0] += NT // 4
            v.wait_ge(dve, steps[0])
            statistics(1)

            def two_z(i):
                wait(v, zT_ready, 2 * i)
                wait(v, z_saved, 32 * i)
                for u in range(2):
                    for j in range(TB):
                        t = bass.ds((2 * i + u) * TB + j, 1)
                        nc.vector.tensor_scalar(z_now[:, u, j, :], xn[:, t, :], mean[:, 1, t], rstd[:, 1, t],
                                                ALU.subtract, ALU.mult).then_inc(z_ready, 1)

            two_z(0)
            with v.Fori(1, B // 2) as i:
                two_z(i)
            v.wait_ge(gates_ready, B)
            v.wait_ge(consts, 1)
            per_e = [P, NT, E]

            def bt(a):
                return a.unsqueeze(2).to_broadcast(per_e)

            rev_b = rev[:].unsqueeze(1).to_broadcast(per_e)
            link(nc.vector.tensor_copy(R["lg"], ps[:, 2, 0:NT * E].rearrange("p (t e) -> p t e", e=E)))
            link(nc.vector.tensor_reduce(r1["m"][:], R["lg"], AX.X, ALU.max))
            nc.vector.tensor_tensor(R["d"], R["lg"], bt(r1["m"][:]), ALU.subtract).then_inc(lg_d, 1)
            v.wait_ge(lg_e, 1)
            link(nc.vector.tensor_reduce(r1["s"][:], R["e"], AX.X, ALU.add))
            link(nc.vector.reciprocal(r1["rs"][:], r1["s"][:]))
            link(nc.vector.tensor_tensor(R["p"], R["e"], bt(r1["rs"][:]), ALU.mult))
            link(nc.vector.tensor_reduce(r1["p1"][:], R["p"], AX.X, ALU.max))
            link(nc.vector.tensor_tensor(R["key"], R["p"], bt(r1["p1"][:]), ALU.is_equal))
            link(nc.vector.tensor_tensor(R["key"], R["key"], rev_b, ALU.mult))
            link(nc.vector.tensor_reduce(r1["k1"][:], R["key"], AX.X, ALU.max))
            link(nc.vector.tensor_tensor(R["oh1"], rev_b, bt(r1["k1"][:]), ALU.is_equal))
            link(nc.vector.scalar_tensor_tensor(out=R["pm"], in0=R["oh1"], scalar=-2.0, in1=R["p"],
                                                op0=ALU.mult, op1=ALU.add))
            link(nc.vector.tensor_reduce(r1["p2"][:], R["pm"], AX.X, ALU.max))
            link(nc.vector.tensor_tensor(R["key"], R["pm"], bt(r1["p2"][:]), ALU.is_equal))
            link(nc.vector.tensor_tensor(R["key"], R["key"], rev_b, ALU.mult))
            link(nc.vector.tensor_reduce(r1["k2"][:], R["key"], AX.X, ALU.max))
            link(nc.vector.tensor_tensor(R["oh2"], rev_b, bt(r1["k2"][:]), ALU.is_equal))
            nc.vector.tensor_tensor(ohb[:].rearrange("p e t -> p t e"), R["oh1"], R["oh2"], ALU.add).then_inc(oh_ready, 1)
            link(nc.vector.scalar_tensor_tensor(out=r1["den"][:], in0=r1["p1"][:], scalar=EPS_TOPK, in1=r1["p2"][:],
                                                op0=ALU.add, op1=ALU.add))
            link(nc.vector.reciprocal(r1["rd"][:], r1["den"][:]))
            link(nc.vector.tensor_tensor(zrow[:, :, D], r1["p1"][:], r1["rd"][:], ALU.mult))
            link(nc.vector.tensor_tensor(w_late[:], r1["p2"][:], r1["rd"][:], ALU.mult))
            v.wait_ge(counts_ready, 1)
            link(nc.vector.tensor_copy(cnt[:], ps[:, 3, :].rearrange("p (a e t) -> p a e t", a=2, e=E)))
            flat = "p e t -> p (e t)"
            link(nc.vector.tensor_tensor_scan(cum[:].rearrange(flat), carry[:].rearrange(flat),
                                              cnt[:, 1].rearrange(flat), 0.0, ALU.mult, ALU.add))
            link(nc.vector.tensor_tensor(cmp[:], cum[:, :, NT - 1:NT].to_broadcast([P, E, NT]),
                                         thr[:].unsqueeze(1).to_broadcast([P, E, NT]), ALU.is_gt))
            link(nc.vector.tensor_reduce(ce[:], cmp[:], AX.X, ALU.add))
            link(nc.vector.tensor_tensor_scan(ends[:], ones_b[:, 0:E], ce[:], 0.0, ALU.mult, ALU.add))
            link(nc.vector.tensor_tensor(starts[:], ends[:], ce[:], ALU.subtract))
            link(nc.vector.tensor_tensor(base[:], cum[:], cnt[:, 1], ALU.subtract))
            link(nc.vector.tensor_tensor(base[:], base[:], cnt[:, 0], ALU.add))
            link(nc.vector.scalar_tensor_tensor(out=base[:], in0=starts[:].unsqueeze(2).to_broadcast([P, E, NT]),
                                                scalar=float(P), in1=base[:], op0=ALU.mult, op1=ALU.add))
            for c in range(2):
                link(nc.vector.tensor_tensor(R["key"], R[f"oh{c + 1}"], base[:].rearrange("p e t -> p t e"), ALU.mult))
                link(nc.vector.tensor_reduce(r1["slf"][:], R["key"], AX.X, ALU.add))
                link(nc.vector.tensor_copy(slot[:, c], r1["slf"][:]))
            v.sem_inc(slots_ready, 1)
            link(nc.vector.tensor_tensor(emap[:], tile_no[:].unsqueeze(2).to_broadcast([P, MAPPED, E]),
                                         ends[:].unsqueeze(1).to_broadcast([P, MAPPED, E]), ALU.is_ge))
            link(nc.vector.tensor_reduce(emap_f[:], emap[:], AX.X, ALU.add))
            nc.vector.tensor_scalar(emap_i[:], emap_f[:], float(E - 1), None, ALU.min).then_inc(map_ready, 1)
            link(nc.vector.tensor_tensor(x_sb[:], x_sb[:], xn[:], ALU.add))
            first = steps[0]


            def queries(b, u, heads=range(4)):
                v.wait_ge(q_ps, b + 1)
                for c in heads:
                    nc.vector.tensor_scalar(qbd[:, u, :, c, :], ps[:, 0, :].rearrange("p (n q) -> p n q", q=QB), cols[:, 0:1],
                                            qmask[:, c:c + 1], ALU.add, ALU.mult).then_inc(q_sb, 1)

            def maxima(b, j):
                v.wait_ge(s_ps, b * PAIRS + j + 1)
                nc.vector.tensor_reduce(negm[:, j % SR], ps[:, 2 + j % SR, :].rearrange("p (c k) -> p c k", k=2 * QB),
                                        AX.X, ALU.max, negate=True).then_inc(m_sb, 1)

            def turned_p(b, j):
                v.wait_ge(p_sb, 8 * (b * PAIRS + j + 1))
                nc.vector.transpose(pT[:, 2 * j:2 * j + 2, :].rearrange("p n c -> p (n c)"), pexp[:, j % SR]).then_inc(pT_sb, 1)

            def invert(b, half):
                if half == 0:
                    v.wait_ge(o_ps, b + 1)
                at = slice(half * S // 2, (half + 1) * S // 2)
                nc.vector.reciprocal(rec[:, at], ps[:, 7, at]).then_inc(rec_sb, 1)

            def normalise(b):
                v.wait_ge(o_out, b + 1)
                v.wait_ge(rec_sb, 2 * (b + 1))
                nc.vector.tensor_tensor(attnT[:], o_now[:], rec[:], ALU.mult).then_inc(o_sb, 1)

            def add(b):
                v.wait_ge(a_ps, b + 1)
                xs = x_sb[:, bass.ds(b * TB, TB), :]
                nc.vector.tensor_tensor(xs, xs, ps[:, 1, :].rearrange("p (t d) -> p t d", t=TB), ALU.add).then_inc(a_sb, 1)

            def sequence(b, u, first, last):
                for j in range(PAIRS):
                    if MAXIMA_FIRST:
                        maxima(b, j)
                    if j >= TURN_LAG:
                        turned_p(b, j - TURN_LAG)
                    elif not first:
                        turned_p(b - 1, PAIRS + j - TURN_LAG)
                    if not MAXIMA_FIRST:
                        maxima(b, j)
                    for part in range(2):
                        if j == DVE_Q[part] and not last:
                            queries(b + 1, 1 - u, (2 * part, 2 * part + 1))
                        if j == DVE_INVERT[part] and not first:
                            invert(b - 1, part)
                    if not first:
                        if j == DVE_NORMALISE:
                            normalise(b - 1)
                        if j == DVE_ADD:
                            add(b - 1)

            v.wait_ge(z_saved, 16 * B)
            v.wait_ge(gates_ready, B)
            queries(0, 0)
            sequence(0, 0, True, False)
            with v.Fori(0, LOOPED) as i:
                for u in range(2):
                    sequence(1 + 2 * i + u, 1 - u, False, False)
            sequence(B - 1, 1, False, True)
            for j in range(PAIRS - TURN_LAG, PAIRS):
                turned_p(B - 1, j)
            invert(B - 1, 0)
            invert(B - 1, 1)
            normalise(B - 1)
            add(B - 1)

            def turned_rows(turn, r):
                k = RING * turn + r
                v.wait_ge(xgT_ps, k + 1)
                wait(v, hT_ps, k - 1)
                nc.vector.tensor_scalar(xgT[:, r % 2], ps[:, 4 + r % 2, 0:P], cols[:, 2:3], cols[:, 3:4],
                                        ALU.mult, ALU.add).then_inc(xgT_sb, 1)

            expert = [v.alloc_register(f"expert{r}") for r in range(RING)]

            def load_experts(turn, half):
                v.load(expert[4 * half:4 * half + 4], emap_i[0:1, bass.ds(RING * turn + 4 * half, 4)])

            def set_weights(turn, r):
                k = RING * turn + r
                e = v.snap(expert[r], min_val=0, max_val=E - 1)
                wait(v, hT_sb, FC * (k - 1))
                nc.vector.tensor_copy(w1_now[:, r % 2], w1_sb[:, bass.ds(e, 1), :].rearrange("p a f -> p (a f)")).then_inc(w1_set, 1)

            def expert_step(turn, r):
                k = RING * turn + r
                if isinstance(k, int) and k >= SLOT_TILES - 1:
                    return
                turned_rows(turn + (r + 1) // RING, (r + 1) % RING)
                set_weights(turn + (r + 1) // RING, (r + 1) % RING)
                if r == 6:
                    load_experts(turn + 1, 1)
                if r == 2:
                    load_experts(turn + 1, 0)

            v.wait_ge(w1_in, 16)
            v.wait_ge(map_ready, 1)
            load_experts(0, 0)
            load_experts(0, 1)
            set_weights(0, 0)
            turned_rows(0, 0)
            run_experts(v, expert_step)
            with v.Fori(0, B // 2) as i:
                for u in range(2):
                    b = 2 * i + u
                    v.wait_ge(y_got[u], 32 * (i + 1))
                    xs = x_sb[:, bass.ds(b * TB, TB), :]
                    nc.vector.tensor_tensor(y_in[:, u, 0], y_in[:, u, 0], y_in[:, u, 1], ALU.add).then_inc(dve, 1)
                    v.wait_ge(dve, first + b + 1)
                    nc.vector.tensor_tensor(xs, xs, y_in[:, u, 0], ALU.add).then_inc(y_sum, 1)

        @block.tensor
        def _(pe):
            mm = nc.tensor.matmul

            def bias(dst, width, at, stop=False):
                return mm(dst, ones_b[0:3, :], b3[:, bass.ds(at, width)], start=True, stop=stop, skip_group_check=True)

            pe.wait_ge(consts, 1)
            pe.wait_ge(wG_in, 32)
            pe.wait_ge(b3_in, 16)

            def two_gates(i):
                for u in range(2):
                    b = 2 * i + u
                    wait(pe, xf_ready, b - 1)
                    for j in range(TB):
                        pe.wait_ge(z_ready, b * TB + j + 1)
                        ins = nc.tensor.transpose(ps[:, u, P * j:P * (j + 1)], z_now[:, u, j, :], ident[:])
                    ins.then_inc(zT_ready, 1)
                for u in range(2):
                    b = 2 * i + u
                    pe.wait_ge(xf_ready, b + 1)
                    for j in range(TB):
                        dst = ps[:, 2, bass.ds((b * TB + j) * E, E)]
                        mm(dst, xfT[:, u, P * j:P * (j + 1)], wG[:], start=True, stop=False, skip_group_check=True)
                        ins = mm(dst, ones_b[0:3, :], b3[:, O_BG:O_BG + E], start=False, stop=True, skip_group_check=True)
                    ins.then_inc(gates_ready, 1)

            two_gates(0)
            with pe.Fori(1, B // 2) as i:
                two_gates(i)
            pe.wait_ge(oh_ready, 1)
            oh = ohb[:].rearrange("p e t -> p (e t)")
            mm(ps[:, 3, 0:E * NT], before[:], oh, start=True, stop=True)
            mm(ps[:, 3, E * NT:2 * E * NT], ones_b[:], oh, start=True, stop=True).then_inc(counts_ready, 1)
            pe.wait_ge(w_in, 16)
            pe.wait_ge(slots_ready, 1)

            def turn_xn(b):
                pe.wait_ge(xnb_in, 16 * (b + 1))
                for j in range(TB):
                    ins = nc.tensor.transpose(ps[:, 0, P * j:P * (j + 1)], xnb[:, j, :], ident[:])
                ins.then_inc(xnT_ps, 1)

            def project_v(b):
                pe.wait_ge(xnT_sb, b + 1)
                mm(ps[:, 0, :], ones_b[0:3, :], b3[:, O_BV:O_BV + D].unsqueeze(1).to_broadcast([3, TB, D]),
                   start=True, stop=False, skip_group_check=True)
                for j in range(TB):
                    ins = mm(ps[:, 0, D * j:D * (j + 1)], xnT[:, P * j:P * (j + 1)],
                             wA[:, 2, :], start=False, stop=(j == TB - 1), skip_group_check=True)
                ins.then_inc(v_ps, 1)

            def project_k(b):
                mm(ps[:, 1, :], wA[:, 1, :], xnT[:], start=True, stop=True).then_inc(k_ps, 1)

            def project_q(b):
                pe.wait_ge(v_sb, 16 * (b + 1))
                mm(ps[:, 0, :], wA[:, 0, :], xnT[:], start=True, stop=True).then_inc(q_ps, 1)

            def scores(b, u, j):
                k = b * PAIRS + j
                wait(pe, p_sb, 8 * (k + 1 - SR))
                if j == 0:
                    pe.wait_ge(k_sb, G * (b + 1))
                    pe.wait_ge(q_sb, 4 * (b + 1))
                first_pair = 0 if j == 0 else 1
                mm(ps[:, 2 + j % SR, :], identb[:], maskS[:, first_pair:first_pair + 2],
                   start=True, stop=False, skip_group_check=True)
                for n in range(2):
                    blk = 2 * j + n
                    ins = mm(ps[:, 2 + j % SR, 256 * n:256 * (n + 1)], qbd[:, u, blk].rearrange("p h q -> p (h q)"),
                             kz[:, u, :, QB * blk:QB * (blk + 2)], start=False, stop=(n == 1), skip_group_check=True)
                ins.then_inc(s_ps, 1)

            def values(u, m):
                wide = 2 if m < NQ - 1 else 1
                for g in range(G):
                    at = (m * 2 * G + 2 * g + 1) * QB
                    apart = (2 * G - 1) * QB
                    if wide == 2:
                        probs = flat_pT[:, at:at + 2 * apart].rearrange("p (a c) -> p a c", a=2)[:, :, 0:QB]
                    else:
                        probs = flat_pT[:, at:at + QB]
                    mm(ps[QB * g:QB * (g + 1), 6, QB * m:QB * (m + wide)], vbd[:, u, m, g, :], probs,
                       start=(m == 0), stop=(m == NQ - 1), skip_group_check=True)

            def denominators(half):
                n0 = half * NQ // 2
                for which in range(2):
                    for g in range(G):
                        ins = mm(ps[QB * g:QB * (g + 1), 7, QB * n0:QB * (n0 + NQ // 2)], vmask[:].rearrange("p h d -> p (h d)"),
                                 pT[:, n0:n0 + NQ // 2, (2 * g + which) * QB:(2 * g + which + 1) * QB],
                                 start=(half == 0 and which == 0), stop=(which == 1), skip_group_check=True)
                return ins

            def weigh(b, u, j):
                pe.wait_ge(pT_sb, b * PAIRS + j + 1)
                if j == 0:
                    wait(pe, o_out, b)
                if j > 0:
                    values(u, 2 * j - 1)
                values(u, 2 * j)
                if j == PAIRS // 2:
                    wait(pe, rec_sb, 2 * b)
                    denominators(0)
                if j == PAIRS - 1:
                    values(u, NQ - 1)
                    denominators(1).then_inc(o_ps, 1)

            def project_out(b):
                pe.wait_ge(o_sb, b + 1)
                mm(ps[:, 1, :], ones_b[0:3, :], b3[:, O_BO:O_BO + D].unsqueeze(1).to_broadcast([3, TB, D]),
                   start=True, stop=False, skip_group_check=True)
                for j in range(TB):
                    ins = mm(ps[:, 1, P * j:P * (j + 1)], attnT[:, P * j:P * (j + 1)], wA[:, 3, :],
                             start=False, stop=(j == TB - 1), skip_group_check=True)
                ins.then_inc(a_ps, 1)

            def sequence(b, u, first, last):
                for j in range(PAIRS):
                    scores(b, u, j)
                    if j >= WEIGH_LAG:
                        weigh(b, u, j - WEIGH_LAG)
                    elif not first:
                        weigh(b - 1, 1 - u, PAIRS + j - WEIGH_LAG)
                    if not last:
                        if j == PE_XN:
                            turn_xn(b + 1)
                        if j == PE_V:
                            project_v(b + 1)
                        if j == PE_K:
                            project_k(b + 1)
                        if j == PE_Q:
                            project_q(b + 1)
                    if j == PE_OUT and not first:
                        if not last:
                            pe.wait_ge(k_sb, G * (b + 2))
                        project_out(b - 1)

            turn_xn(0)
            project_v(0)
            project_k(0)
            project_q(0)
            sequence(0, 0, True, False)
            with pe.Fori(0, LOOPED) as i:
                for u in range(2):
                    sequence(1 + 2 * i + u, 1 - u, False, False)
            sequence(B - 1, 1, False, True)
            for j in range(PAIRS - WEIGH_LAG, PAIRS):
                weigh(B - 1, 1, j)
            project_out(B - 1)
            pe.wait_ge(w2_in, 16)

            def turn_rows(turn, r):
                k = RING * turn + r
                pe.wait_ge(xg_in[r], 16 * (turn + 1))
                wait(pe, xgT_sb, k - 1)
                nc.tensor.transpose(ps[:, 4 + r % 2, 0:P], xg[:, r, 0:D], ident[:]).then_inc(xgT_ps, 1)

            expert = [pe.alloc_register(f"expert{r}") for r in range(RING)]

            def load_experts(turn, half):
                pe.load(expert[4 * half:4 * half + 4], emap_i[0:1, bass.ds(RING * turn + 4 * half, 4)])

            def expert_step(turn, r):
                k = RING * turn + r
                start, last = (isinstance(k, int) and k == n for n in (0, SLOT_TILES))
                if not last:
                    if not (isinstance(k, int) and k == SLOT_TILES - 1):
                        turn_rows(turn + (r + 1) // RING, (r + 1) % RING)
                    pe.wait_ge(xgT_sb, k + 1)
                    pe.wait_ge(w1_set, k + 1)
                    wait(pe, hT_sb, FC * (k - 1))
                    for c in range(FC):
                        ins = mm(ps[:, r % 2, P * c:P * (c + 1)], w1_now[:, r % 2, P * c:P * (c + 1)], xgT[:, r % 2, :],
                                 start=True, stop=True, skip_group_check=True)
                    ins.then_inc(hT_ps, 1)
                if not start:
                    before = (r - 1) % RING
                    e = pe.snap(expert[before], min_val=0, max_val=E - 1)
                    wait(pe, y_sb, k - 2)
                    bias(ps[:, 6 + before % 2, 0:D], D, e * D + O_B2)
                    pe.wait_ge(hT_sb, FC * k)
                    for c in range(FC):
                        ins = mm(ps[:, 6 + before % 2, 0:D], hT[:, before % 2, c, :],
                                 w2_sb[:, bass.ds(e * FC + c, 1), :], start=False, stop=(c == FC - 1), skip_group_check=True)
                    ins.then_inc(y_ps, 1)
                    if r == 0:
                        load_experts(turn, 1)
                    if r == 4:
                        load_experts(turn + 1, 0)

            pe.wait_ge(map_ready, 1)
            load_experts(0, 0)
            load_experts(0, 1)
            turn_rows(0, 0)
            run_experts(pe, expert_step)


def kernel(**inputs):
    import numpy as np
    import concourse.bacc as bacc
    from concourse.bass_utils import run_bass_kernel_spmd

    a = {k[3:]: np.asarray(v) for k, v in inputs.items()}
    E, DF, D = a["ffn_W1"].shape
    w_attn = np.stack([a["attn_W" + n].T for n in "qkvo"], axis=1)
    b_cols = np.stack([a["attn_bq"], a["attn_bk"], a["ffn_gamma"], a["ffn_beta"]], axis=1)
    rows = np.concatenate([a["ffn_b2"].ravel(), a["attn_bo"], a["attn_bv"], a["ffn_bg"]])
    width = -(-rows.size // 128) * 128
    bias_rows = np.zeros((1, width), rows.dtype)
    bias_rows[0, :rows.size] = rows
    w1 = np.concatenate([a["ffn_W1"].transpose(2, 0, 1), a["ffn_b1"].reshape(E, DF // 128, 128).transpose(2, 0, 1)], axis=2)
    w2 = a["ffn_W2"].transpose(2, 0, 1).reshape(DF // 128, 128, E, D).transpose(1, 2, 0, 3).reshape(128, E * (DF // 128), D)
    ins = {"x": a["attn_x"], "w_attn": w_attn, "b_cols": b_cols, "bias_rows": bias_rows,
           "w_gate": a["ffn_Wg"].T, "w1": w1, "w2": w2}
    ins = {k: np.ascontiguousarray(v) for k, v in ins.items()}

    nc = bacc.Bacc("TRN2", target_bir_lowering=False, num_devices=1)
    args = [nc.dram_tensor("in_" + k, v.shape, F32, kind="ExternalInput").ap() for k, v in ins.items()]
    out = nc.dram_tensor("out", a["attn_x"].shape, F32, kind="ExternalOutput").ap()
    attention_and_experts(nc, *args, out)
    got = run_bass_kernel_spmd(nc, [{"in_" + k: v for k, v in ins.items()}], core_ids=[0])
    return got.results[0]["out"]
```

```python
from contextlib import ExitStack

import concourse.bass as bass
from concourse import mybir

F32 = mybir.dt.float32
BF16 = mybir.dt.bfloat16
I32 = mybir.dt.int32
ALU = mybir.AluOpType
ACT = mybir.ActivationFunctionType
AX = mybir.AxisListType

P = 128
NEG = -1.0e30
EPS_LN = 1e-5
EPS_TOPK = 1e-8


def attention_and_experts(nc, x, w_attn, b_cols, bias_rows, w_gate, w1, w2, out):
    B, S, D = x.shape
    TB = S // P
    NT = B * TB
    TOKENS = NT * P
    E = w_gate.shape[1]
    DF = w1.shape[2] * P // (P + 1)
    FC = DF // P
    W1C = DF + FC
    DH = 8
    QB = 32
    NQ = S // QB
    G = 4
    SLOT_TILES = 2 * NT + E - 1
    SLOTS = (SLOT_TILES + 1) * P
    MAPPED = SLOT_TILES + 9
    ROW = D + 2
    RING = 8
    SR = 4
    TURN_LAG, WEIGH_LAG = 2, 3
    YRING = 4
    NB = bias_rows.shape[1]
    O_B2, O_BO, O_BV, O_BG = 0, E * D, E * D + D, E * D + 2 * D
    NBC = NB // P

    xg_dram = nc.dram_tensor("slot_rows", (SLOTS, ROW), F32, kind="Internal").ap()
    y_dram = nc.dram_tensor("expert_rows", (2 * TOKENS, D), F32, kind="Internal").ap()
    b3_dram = nc.dram_tensor("bias_parts", (3, NB), BF16, kind="Internal").ap()

    with ExitStack() as ctx:
        def sb(name, shape, dt=F32):
            return ctx.enter_context(nc.sbuf_tensor(name, shape, dt))

        def sem(name):
            return ctx.enter_context(nc.semaphore(name))

        x_sb = sb("x_sb", [P, NT, D])
        xn = sb("xn", [P, NT, D])
        zrow = sb("zrow", [P, NT, ROW])
        w_late = sb("w_late", [P, NT])
        row_late = sb("row_late", [P, NT], I32)
        ident = sb("ident", [P, P])
        identb = sb("identb", [P, P], BF16)
        ones_b = sb("ones_b", [P, P], BF16)
        before = sb("before", [P, P], BF16)
        maskS = sb("maskS", [P, 3, G, 2 * QB], BF16)
        qmask = sb("qmask", [P, 4])
        vmask = sb("vmask", [P, 4, DH])
        window = sb("window", [P, 2 * QB])
        zeros = sb("zeros", [P, 8, ROW])
        wA = sb("wA", [P, 4, D])
        wG = sb("wG", [P, E])
        w1_sb = sb("w1_sb", [P, E, W1C])
        w2_sb = sb("w2_sb", [P, E * FC, D])
        cols = sb("cols", [P, 4])
        b_in = sb("b_in", [P, NBC])
        b_res = sb("b_res", [P, NBC])
        b_part = sb("b_part", [P, 3, NBC], BF16)
        b3 = sb("b3", [3, NB], BF16)
        st = sb("st", [P, NT, 6])
        mean = sb("mean", [P, NT])
        offset = sb("offset", [P, NT])
        rstd = sb("rstd", [P, 2, NT])
        lw = sb("lw", [P, 8, NT])
        r1 = {n: sb("s_" + n, [P, NT]) for n in ("m", "s", "rs", "p1", "k1", "p2", "k2", "den", "rd", "slf")}
        rev = sb("rev", [P, E])
        carry = sb("carry", [P, E, NT])
        thr = sb("thr", [P, NT])
        tile_no = sb("tile_no", [P, MAPPED])
        ohb = sb("ohb", [P, E, NT], BF16)
        cnt = sb("cnt", [P, 2, E, NT])
        cum = sb("cum", [P, E, NT])
        base = sb("base", [P, E, NT])
        cmp = sb("cmp", [P, E, NT])
        ce = sb("ce", [P, E])
        ends = sb("ends", [P, E])
        starts = sb("starts", [P, E])
        emap = sb("emap", [P, MAPPED, E])
        emap_f = sb("emap_f", [P, MAPPED])
        emap_i = sb("emap_i", [P, MAPPED], I32)
        slot = sb("slot", [P, 2, NT], I32)
        xnb = sb("xnb", [P, TB, D])
        xnT = sb("xnT", [P, S])
        qbd = sb("qbd", [P, 2, NQ, 4, QB])
        kz = sb("kz", [P, 2, G, QB + S])
        vbd = sb("vbd", [P, 2, NQ, G, 4 * DH])
        negm = sb("negm", [P, SR, 8])
        pexp = sb("pexp", [P, SR, S])
        pT_all = sb("pT", [P, NQ + 1, 2 * G * QB])
        pT = pT_all[:, 0:NQ]
        q_now = sb("q_now", [P, S])
        ends_of_b = sb("ends_of_b", [P, 3, S])
        rec, o_now, attnT = (ends_of_b[:, n] for n in range(3))
        flat_w2 = w2_sb[:].rearrange("p a d -> p (a d)")
        flat_pT = pT_all[:].rearrange("p n c -> p (n c)")
        R = {n: flat_w2[:, NT * E * k:NT * E * (k + 1)].rearrange("p (t e) -> p t e", e=E)
             for k, n in enumerate(("lg", "d", "e", "p", "key", "oh1", "oh2", "pm"))}
        flat_vbd = vbd[:].rearrange("p u n g d -> p (u n g d)")
        y_in = [half[:, 2 * S * k:2 * S * (k + 1)] for half in (flat_pT, flat_vbd) for k in range(B // 2)]
        z_now = qbd[:, 1].rearrange("p n h q -> p (n h q)").rearrange("p (u t d) -> p u t d", u=4, t=TB)
        xfT = ends_of_b[:, 0:2]
        xg = sb("xg", [P, RING, ROW])
        flat_kz = kz[:].rearrange("p u g k -> p (u g k)")
        O_W, O_X, O_Y = 2 * DF, 2 * DF + 2 * W1C, 2 * DF + 2 * W1C + 2 * P
        hT = flat_kz[:, 0:O_W].rearrange("p (u c t) -> p u c t", u=2, c=FC)
        w1_now = flat_kz[:, O_W:O_X].rearrange("p (u f) -> p u f", u=2)
        xgT = flat_kz[:, O_X:O_Y].rearrange("p (u t) -> p u t", u=2)
        y = flat_kz[:, O_Y:O_Y + YRING * D].rearrange("p (u d) -> p u d", u=YRING)
        ps = ctx.enter_context(nc.psum_tensor("ps", [P, 8, 512], F32))

        x_in = [sem(f"x_in{n}") for n in range(4)]
        w_in = sem("w_in"); wG_in = sem("wG_in"); cols_in = sem("cols_in"); w1_in = sem("w1_in"); w2_in = sem("w2_in")
        b_got = sem("b_got"); b_put = sem("b_put"); b3_in = sem("b3_in"); b_done = sem("b_done")
        zero_put = sem("zero_put")
        pool = sem("pool")
        idents = sem("idents")
        masks = sem("masks")
        consts = sem("consts")
        mean_ready = sem("mean_ready")
        cleared = sem("cleared")
        vbd_clear = sem("vbd_clear")
        lg_out = sem("lg_out"); cnt_out = sem("cnt_out"); x_plus = sem("x_plus")
        dve = sem("dve")
        var_ready = sem("var_ready"); std_ready = sem("std_ready"); z_scale = sem("z_scale")
        xn_ready = sem("xn_ready"); xn_late = sem("xn_late")
        z_ready = sem("z_ready"); zT_ready = sem("zT_ready"); z_saved = [sem(f"z_saved{n}") for n in range(2)]
        xf_ready = sem("xf_ready"); gates_ready = sem("gates_ready")
        lg_d = sem("lg_d"); lg_e = sem("lg_e")
        oh_ready = sem("oh_ready"); counts_ready = sem("counts_ready")
        slots_ready = sem("slots_ready"); map_ready = sem("map_ready")
        sent = sem("sent")
        xnb_in = sem("xnb_in"); xnT_ps = sem("xnT_ps"); xnT_sb = sem("xnT_sb")
        q_ps = sem("q_ps"); q_out = sem("q_out"); k_ps = sem("k_ps"); q_sb = sem("q_sb"); k_sb = sem("k_sb")
        v_ps = sem("v_ps"); v_sb = sem("v_sb")
        s_ps = sem("s_ps"); m_sb = sem("m_sb"); p_sb = sem("p_sb"); pT_sb = sem("pT_sb")
        o_ps = sem("o_ps"); o_out = sem("o_out"); o_sb = sem("o_sb"); rec_sb = sem("rec_sb")
        a_ps = sem("a_ps"); a_sb = sem("a_sb")
        xg_in = [sem(f"xg_in{n}") for n in range(RING)]
        xgT_ps = sem("xgT_ps"); xgT_sb = sem("xgT_sb"); w1_set = sem("w1_set")
        hT_ps = sem("hT_ps"); hT_sb = sem("hT_sb"); y_ps = sem("y_ps"); y_sb = sem("y_sb"); y_going = sem("y_going")
        y_put = [sem(f"y_put{n}") for n in range(RING)]
        y_got = [sem(f"y_got{n}") for n in range(B)]
        y_sum = [sem(f"y_sum{b}") for b in range(B)]; y_half = sem("y_half"); out_put = sem("out_put")

        block = ctx.enter_context(nc.Block())
        LATE = 5 * TB
        X_LOADS = ((0, TB), (TB, 3 * TB), (3 * TB, 5 * TB), (5 * TB, NT))
        x_tiles = x.rearrange("b (t p) d -> p (b t) d", p=P)
        out_tiles = out.rearrange("b (t p) d -> p (b t) d", p=P)
        xg_tiles = xg_dram.rearrange("(i p) c -> p i c", p=P)
        y_rows = y_dram.rearrange("(b p n) d -> p b (n d)", b=B, p=P)

        PAIRS = NQ // 2
        PE_XN, PE_V, PE_K, PE_Q, PE_OUT = 0, 2, 4, 5, 7
        ACT_Q = 5
        ACT_QUADRANTS = 3
        DVE_V = (3, 4)
        ACT_XN, ACT_V, ACT_K, ACT_O = 0, (2, 3), (5, 5), 2
        DVE_INVERT, DVE_ADD = (2, 4), 6
        SENT_AT_A_TIME = 13
        ROUTE_FROM, PARTS = 4, 11
        COUNTS_AT = 2
        GPSIMD_SUMS = (3, 6)
        LOOPED = (B - 4) // 2
        FIRST = RING - 2
        OUT_AT, INVERT_AT, ADD_AT = 3, (0, 1), 4
        TURNS = (SLOT_TILES - 1 - FIRST) // RING

        def wait(engine, semaphore, count):
            if not isinstance(count, int) or count > 0:
                engine.wait_ge(semaphore, count)

        def run_experts(engine, step, last_of_attention=()):
            for r in range(FIRST):
                step(0, r)
                for at, what in last_of_attention:
                    if at == r:
                        what()
            with engine.Fori(0, TURNS) as i:
                for r in range(FIRST, FIRST + RING):
                    step(i + r // RING, r % RING)
            for k in range(SLOT_TILES - 1, SLOT_TILES + 1):
                step(k // RING, k % RING)

        def summands(b):
            y_of_b = y_in[b].rearrange("p (t c d) -> p t c d", t=TB, c=2)
            return x_sb[:, b * TB:(b + 1) * TB, :], y_of_b[:, :, 0], y_of_b[:, :, 1]

        def v_part(n, c):
            return ps[QB * n:QB * (n + 1), 0, :].rearrange("p (t g h d) -> p t g h d", t=TB, g=G, h=4)[:, :, :, c, :]

        def v_diag(u, n, c):
            return vbd[QB * c:QB * (c + 1), u].rearrange("p (t n) g d -> p t n g d", n=4)[:, :, n, :, DH * c:DH * (c + 1)]

        @block.sync
        def _(sp):
            for n, (t0, t1) in enumerate(X_LOADS):
                sp.dma_start(x_sb[:, t0:t1, :], x_tiles[:, t0:t1, :]).then_inc(x_in[n], 16)
                if n == 0:
                    sp.dma_start(wA[:], w_attn).then_inc(w_in, 16)
                    sp.dma_start(b_in[:], bias_rows.rearrange("a (p c) -> (a p) c", p=P)).then_inc(b_got, 16)
                    sp.dma_start(cols[:], b_cols).then_inc(cols_in, 16)
                    sp.dma_start(wG[:], w_gate).then_inc(wG_in, 16)
            sp.wait_ge(xn_ready, TB)
            sp.dma_start(xnb[:], xn[:, 0:TB, :]).then_inc(xnb_in, 16)
            sp.wait_ge(b_done, 1)
            sp.dma_start(b3_dram.rearrange("a (p c) -> p a c", p=P), b_part[:]).then_inc(b_put, 16)
            sp.wait_ge(b_put, 16)
            sp.dma_start(b3[:], b3_dram).then_inc(b3_in, 16)
            for n in range(B // 2):
                sp.wait_ge(z_ready, 2 * (n + 1))
                sp.dma_start(zrow[:, 2 * TB * n:2 * TB * (n + 1), 0:D],
                             z_now[:, 2 * (n % 2):2 * (n % 2) + 2].rearrange("p u t d -> p (u t) d")).then_inc(z_saved[n % 2], 16)
                if n == 0:
                    sp.wait_ge(xnT_ps, 1)
                    sp.wait_ge(xn_ready, 2 * TB)
                    sp.dma_start(xnb[:], xn[:, TB:2 * TB, :]).then_inc(xnb_in, 16)
            sp.dma_start(w1_sb[:], w1).then_inc(w1_in, 16)
            sp.wait_ge(xn_late, NT - LATE)
            sp.wait_ge(consts, 1)
            for n in range(SLOTS // P // 8):
                sp.dma_start(xg_tiles[:, 8 * n:8 * (n + 1), :], zeros[:]).then_inc(zero_put, 16)
            sp.wait_ge(xnT_ps, 2)
            sp.dma_start(xnb[:], xn[:, 2 * TB:3 * TB, :]).then_inc(xnb_in, 16)
            sp.wait_ge(xnT_ps, 3)
            sp.dma_start(xnb[:], xn[:, 3 * TB:4 * TB, :]).then_inc(xnb_in, 16)
            sp.wait_ge(slots_ready, 1)
            sp.dma_start(w2_sb[:], w2).then_inc(w2_in, 16)
            with sp.Fori(4, B) as b:
                sp.wait_ge(xnT_ps, b)
                sp.dma_start(xnb[:], xn[:, bass.ds(b * TB, TB), :]).then_inc(xnb_in, 16)
            sp.wait_ge(sent, 16 * 2 * NT)
            for n in range(RING):
                sp.dma_start(xg[:, n, :], xg_tiles[:, n, :]).then_inc(xg_in[n], 16)

            def next_rows(i, n):
                sp.wait_ge(y_put[n], 16 * i)
                sp.dma_start(xg[:, n, :], xg_tiles[:, bass.ds(RING * i + n, 1), :]).then_inc(xg_in[n], 16)

            with sp.Fori(1, SLOT_TILES // RING) as i:
                for n in range(RING):
                    next_rows(i, n)
            for n in range(SLOT_TILES % RING):
                next_rows(SLOT_TILES // RING, n)
            for n in range(RING):
                sp.wait_ge(y_put[n], 16 * len(range(n, SLOT_TILES, RING)))
            for b in range(B):
                sp.dma_start(y_in[b], y_rows[:, b, :]).then_inc(y_got[b], 16)

        @block.gpsimd
        def _(gp):
            steps = [0]

            def step(ins):
                steps[0] += 1
                ins.then_inc(pool, 1)
                gp.wait_ge(pool, steps[0])

            step(nc.gpsimd.memset(ident[:], 0.0))
            step(nc.gpsimd.affine_select(out=ident[:], in_=ident[:], compare_op=ALU.not_equal, fill=1.0, base=0,
                             pattern=[[-1, P]], channel_multiplier=1))
            step(nc.gpsimd.memset(ones_b[:], 1.0))
            step(nc.gpsimd.tensor_copy(identb[:], ident[:]))
            gp.sem_inc(idents, 1)
            step(nc.gpsimd.memset(qmask[:], float(DH) ** -0.5))
            step(nc.gpsimd.memset(vmask[:], 1.0))
            step(nc.gpsimd.memset(window[:], 0.0))
            step(nc.gpsimd.affine_select(out=vmask[:], in_=vmask[:], compare_op=ALU.is_ge, fill=0.0, base=0,
                             pattern=[[-32, 4], [0, DH]], channel_multiplier=1))
            step(nc.gpsimd.affine_select(out=vmask[:], in_=vmask[:], compare_op=ALU.is_ge, fill=0.0, base=31,
                             pattern=[[32, 4], [0, DH]], channel_multiplier=-1))
            for j in range(4):
                part = slice(32 * j, 32 * j + 32)
                step(nc.gpsimd.affine_select(out=qmask[part, :], in_=qmask[part, :], compare_op=ALU.is_ge, fill=0.0, base=0,
                                 pattern=[[-DH, 4]], channel_multiplier=1))
                step(nc.gpsimd.affine_select(out=window[part], in_=window[part], compare_op=ALU.is_ge, fill=NEG, base=-1,
                                 pattern=[[1, 2 * QB]], channel_multiplier=-1))
            for j in range(4):
                part = slice(32 * j, 32 * j + 32)
                step(nc.gpsimd.affine_select(out=qmask[part, :], in_=qmask[part, :], compare_op=ALU.is_ge, fill=0.0, base=DH - 1,
                                 pattern=[[DH, 4]], channel_multiplier=-1))
                step(nc.gpsimd.affine_select(out=window[part], in_=window[part], compare_op=ALU.is_ge, fill=NEG, base=QB,
                                 pattern=[[-1, 2 * QB]], channel_multiplier=1))
            step(nc.gpsimd.tensor_copy(maskS[:].rearrange("p a g k -> p (a g) k"),
                                       window[:].unsqueeze(1).to_broadcast([P, 3 * G, 2 * QB])))
            step(nc.gpsimd.memset(maskS[:, 0, :, 0:QB], NEG))
            gp.sem_inc(masks, 1)
            nc.gpsimd.memset(vbd[:], 0.0).then_inc(vbd_clear, 1)

            gp.wait_ge(z_scale, 1)

            def two_z(i, u):
                if isinstance(i, int) and i == 0:
                    gp.wait_ge(xn_ready, 2 * TB * (u + 1))
                else:
                    gp.wait_ge(xn_ready, LATE)
                    gp.wait_ge(xn_late, NT - LATE)
                for w in range(2):
                    t = bass.ds((2 * (2 * i + u) + w) * TB, TB)
                    nc.gpsimd.tensor_tensor(z_now[:, 2 * u + w], xn[:, t, :],
                                            rstd[:, 1, t].unsqueeze(2).to_broadcast([P, TB, D]), ALU.mult).then_inc(z_ready, 1)

            for u in range(2):
                two_z(0, u)
            with gp.Fori(1, B // 4) as i:
                for u in range(2):
                    gp.wait_ge(zT_ready, 2 * (2 * i + u - 1))
                    gp.wait_ge(z_saved[u], 16 * i)
                    two_z(i, u)
            step(nc.gpsimd.memset(before[:], 1.0))
            step(nc.gpsimd.memset(zeros[:], 0.0))
            step(nc.gpsimd.memset(carry[:], 1.0))
            step(nc.gpsimd.iota(rev[:], [[-1, E]], base=E, channel_multiplier=0, allow_small_or_imprecise_dtypes=True))
            step(nc.gpsimd.iota(thr[:], [[P, NT]], base=0, channel_multiplier=0, allow_small_or_imprecise_dtypes=True))
            step(nc.gpsimd.iota(tile_no[:], [[1, MAPPED]], base=0, channel_multiplier=0, allow_small_or_imprecise_dtypes=True))
            step(nc.gpsimd.iota(zrow[:, :, D + 1].bitcast(I32), [[2 * S, B], [2, TB]], base=0, channel_multiplier=2 * TB))
            step(nc.gpsimd.iota(row_late[:], [[2 * S, B], [2, TB]], base=1, channel_multiplier=2 * TB))
            step(nc.gpsimd.affine_select(out=before[:], in_=before[:], compare_op=ALU.is_gt, fill=0.0, base=0,
                             pattern=[[1, P]], channel_multiplier=-1))
            step(nc.gpsimd.memset(carry[:, :, 0:1], 0.0))
            step(nc.gpsimd.iota(zeros[:, :, D + 1].bitcast(I32), [[0, 8]], base=2 * TOKENS, channel_multiplier=1))
            gp.sem_inc(consts, 1)


            def queries(b, u):
                gp.wait_ge(q_out, b + 1)
                if b == 1:
                    for n in range(2):
                        gp.wait_ge(z_saved[n], 16 * (B // 4))
                for c in range(4):
                    nc.gpsimd.tensor_tensor(qbd[:, u, :, c, :], q_now[:].rearrange("p (n q) -> p n q", q=QB),
                                            qmask[:, c:c + 1].unsqueeze(2).to_broadcast([P, NQ, QB]), ALU.mult).then_inc(q_sb, 1)

            def normalise(b):
                gp.wait_ge(rec_sb, 2 * (b + 1))
                gp.wait_ge(o_out, b + 1)
                nc.gpsimd.tensor_tensor(attnT, o_now, rec, ALU.mult).then_inc(o_sb, 1)

            def add_xn(b):
                at = slice(b * TB, (b + 1) * TB)
                nc.gpsimd.tensor_tensor(x_sb[:, at, :], x_sb[:, at, :], xn[:, at, :], ALU.add).then_inc(x_plus, 1)

            def scatter(first, last):
                for k in range(first, last):
                    c, t = divmod(k, NT)
                    if k == 0:
                        gp.wait_ge(zero_put, 16 * (SLOTS // P // 8))
                        gp.wait_ge(slots_ready, 1)
                    if k == NT:
                        gp.wait_ge(sent, 16 * NT)
                        step(nc.gpsimd.tensor_copy(zrow[:, :, D], w_late[:]))
                        step(nc.gpsimd.tensor_copy(zrow[:, :, D + 1].bitcast(I32), row_late[:]))
                    gp.indirect_dma_start(xg_dram, bass.IndirectOffsetOnAxis(ap=slot[:, c, t:t + 1], axis=0),
                                          zrow[:, t, :], None).then_inc(sent, 16)

            for b in range(B // 2):
                add_xn(b)
            queries(1, 1)
            for b in range(B // 2, B):
                add_xn(b)
            rows_sent = 0
            for b in range(1, B):
                normalise(b - 1)
                if b + 1 < B:
                    queries(b + 1, (b + 1) % 2)
                more = min(SENT_AT_A_TIME, 2 * NT - rows_sent) if b > 1 else 0
                scatter(rows_sent, rows_sent + more)
                rows_sent += more
            normalise(B - 1)
            last_row = gp.to_reg(2 * TOKENS - 1)

            def result(i, n):
                gp.wait_ge(y_sb, RING * i + n + 1)
                gp.sem_inc(y_going, 1)
                gp.indirect_dma_start(y_dram, bass.IndirectOffsetOnAxis(ap=xg[:, n, D + 1:D + 2].bitcast(I32), axis=0),
                                      y[:, n % YRING, :], None, bounds_check=last_row, oob_is_err=False).then_inc(y_put[n], 16)

            with gp.Fori(0, SLOT_TILES // RING) as i:
                for n in range(RING):
                    result(i, n)
            for n in range(SLOT_TILES % RING):
                result(SLOT_TILES // RING, n)
            for n, b in enumerate(GPSIMD_SUMS):
                gp.wait_ge(y_got[b], 16)
                gp.wait_ge(a_sb, B)
                xs, first_choice, second_choice = summands(b)
                nc.gpsimd.tensor_tensor(xs, xs, first_choice, ALU.add).then_inc(y_half, 1)
                gp.wait_ge(y_half, n + 1)
                nc.gpsimd.tensor_tensor(xs, xs, second_choice, ALU.add).then_inc(y_sum[b], 1)

        @block.scalar
        def _(act):
            def two_xf(i):
                for u in range(2):
                    act.wait_ge(zT_ready, 2 * i + u + 1)
                    wait(act, gates_ready, 2 * i + u - 1)
                    nc.scalar.activation(xfT[:, u], ps[:, 6 + u, :], ACT.Identity, bias=cols[:, 3:4],
                                         scale=cols[:, 2:3]).then_inc(xf_ready, 1)

            def router_exponentials():
                act.wait_ge(lg_d, 1)
                nc.scalar.activation(R["e"], R["d"], ACT.Exp).then_inc(lg_e, 1)

            def turned_xn(b):
                act.wait_ge(xnT_ps, b + 1)
                nc.scalar.activation(xnT[:], ps[:, 0, :], ACT.Copy).then_inc(xnT_sb, 1)

            def queries(b, bank=0):
                act.wait_ge(q_ps, b + 1)
                nc.scalar.activation(q_now[:], ps[:, bank, :], ACT.Identity, bias=cols[:, 0:1]).then_inc(q_out, 1)

            def keys(b, u, groups=range(G)):
                act.wait_ge(k_ps, b + 1)
                for g in groups:
                    q = slice(32 * g, 32 * g + 32)
                    nc.scalar.activation(kz[q, u, g, QB:QB + S], ps[q, 1, :], ACT.Identity,
                                         bias=cols[q, 1:2]).then_inc(k_sb, 1)

            def values(b, u, quadrants):
                if quadrants:
                    act.wait_ge(v_ps, b + 1)
                for n in quadrants:
                    for c in range(4):
                        nc.scalar.activation(v_diag(u, n, c), v_part(n, c), ACT.Copy).then_inc(v_sb, 1)

            def deviations(n, t0, t1):
                act.wait_ge(var_ready, n + 1)
                nc.scalar.activation(lw[:, 7, t0:t1], lw[:, 6, t0:t1], ACT.Sqrt).then_inc(std_ready, 1)

            deviations(0, 0, TB)
            act.wait_ge(cols_in, 16)
            act.wait_ge(cleared, 1)
            turned_xn(0)
            queries(0, 4)
            deviations(1, TB, NT)
            keys(0, 0)
            deviations(2, 0, NT)
            act.wait_ge(mean_ready, 1)
            for t in range(LATE, NT):
                nc.scalar.activation(xn[:, t, :], x_sb[:, t, :], ACT.Identity, bias=offset[:, t:t + 1],
                                     scale=rstd[:, 0, t:t + 1]).then_inc(xn_late, 1)
            act.wait_ge(vbd_clear, 1)

            def exponentials(b, j):
                k = b * PAIRS + j
                act.wait_ge(m_sb, k + 1)
                wait(act, pT_sb, k + 1 - SR)
                for c in range(8):
                    nc.scalar.activation(pexp[:, j % SR, 64 * c:64 * c + 64], ps[:, 2 + j % SR, 64 * c:64 * c + 64],
                                         ACT.Exp, bias=negm[:, j % SR, c:c + 1]).then_inc(p_sb, 1)

            def values_out(b):
                act.wait_ge(o_ps, b + 1)
                wait(act, o_sb, b)
                nc.scalar.activation(o_now, ps[:, 6, :], ACT.Copy).then_inc(o_out, 1)

            def sequence(b, u, first, last):
                for j in range(PAIRS):
                    exponentials(b, j)
                    if first and j < B // 2:
                        two_xf(j)
                    if first and j == ROUTE_FROM:
                        router_exponentials()
                    if j == ACT_Q and not last:
                        queries(b + 1)
                    if j == ACT_O and not first:
                        values_out(b - 1)
                    if last:
                        continue
                    if j == ACT_XN:
                        turned_xn(b + 1)
                    for part in range(2):
                        if j == ACT_V[part]:
                            values(b + 1, 1 - u, range(ACT_QUADRANTS)[part::2])
                        if j == ACT_K[part]:
                            keys(b + 1, 1 - u, (2 * part, 2 * part + 1))

            values(0, 0, range(2))
            sequence(0, 0, True, False)
            sequence(1, 1, False, False)
            with act.Fori(0, LOOPED) as i:
                for u in range(2):
                    sequence(2 + 2 * i + u, u, False, False)
            sequence(B - 2, 0, False, False)
            sequence(B - 1, 1, False, True)
            values_out(B - 1)
            act.wait_ge(s_ps, B * PAIRS)

            def expert_step(turn, r):
                k = RING * turn + r
                last = isinstance(k, int) and k == SLOT_TILES
                if not last:
                    act.wait_ge(hT_ps, k + 1)
                    wait(act, y_ps, k - 1)
                    for c in range(FC):
                        nc.scalar.activation(hT[:, r % 2, c], ps[:, r % 2, P * c:P * (c + 1)], ACT.Gelu,
                                             bias=w1_now[:, r % 2, DF + c:DF + c + 1]).then_inc(hT_sb, 1)
                if isinstance(k, int) and k == 0:
                    return
                before = (r - 1) % RING
                act.wait_ge(y_ps, k)
                wait(act, y_put[(r - 1 - YRING) % RING], 16 * (turn + (r - 1 - YRING) // RING + 1))
                nc.scalar.activation(y[:, before % YRING, :], ps[:, 2 + before % 2, 0:D], ACT.Copy,
                                     scale=xg[:, before, D:D + 1]).then_inc(y_sb, 1)

            run_experts(act, expert_step)
            for b in range(B):
                act.wait_ge(y_sum[b], 1)
                act.dma_start(out_tiles[:, b * TB:(b + 1) * TB, :], x_sb[:, b * TB:(b + 1) * TB, :]).then_inc(out_put, 16)
            act.wait_ge(out_put, 16 * B)

        @block.vector
        def _(v):
            steps = [0]

            def link(ins):
                steps[0] += 1
                ins.then_inc(dve, 1)
                v.wait_ge(dve, steps[0])

            nc.vector.memset(kz[:], 0.0).then_inc(cleared, 1)
            def inverse_root(n, out, t0, t1):
                a = lw[:, :, t0:t1]
                v.wait_ge(std_ready, n + 1)
                link(nc.vector.reciprocal(a[:, 0], a[:, 7]))
                link(nc.vector.tensor_tensor(a[:, 1], a[:, 0], a[:, 0], ALU.mult))
                link(nc.vector.tensor_tensor(a[:, 2], a[:, 1], a[:, 6], ALU.mult))
                link(nc.vector.tensor_scalar(a[:, 3], a[:, 2], -0.5, 1.5, ALU.mult, ALU.add))
                return nc.vector.tensor_tensor(rstd[:, out, t0:t1], a[:, 3], a[:, 0], ALU.mult)

            def statistics(n, t0, t1):
                me, mo, qe, qo = (st[:, t0:t1, k] for k in (1, 4, 2, 5))
                a = lw[:, :, t0:t1]
                link(nc.vector.tensor_tensor(a[:, 0], me, mo, ALU.subtract))
                link(nc.vector.tensor_tensor(a[:, 1], qe, qo, ALU.add))
                link(nc.vector.tensor_tensor(a[:, 2], a[:, 0], a[:, 0], ALU.mult))
                link(nc.vector.tensor_scalar(a[:, 3], a[:, 1], 1.0 / D, None, ALU.mult))
                link(nc.vector.scalar_tensor_tensor(out=a[:, 5], in0=a[:, 2], scalar=0.25, in1=a[:, 3],
                                                    op0=ALU.mult, op1=ALU.add))
                nc.vector.tensor_scalar(a[:, 6], a[:, 5], EPS_LN, None, ALU.add).then_inc(var_ready, 1)
                link(nc.vector.tensor_tensor(a[:, 4], me, mo, ALU.add))
                link(nc.vector.tensor_scalar(mean[:, t0:t1], a[:, 4], 0.5, None, ALU.mult))
                link(inverse_root(n, 0, t0, t1))

            def normalise_x(t):
                nc.vector.tensor_scalar(xn[:, t, :], x_sb[:, t, :], mean[:, t], rstd[:, 0, t],
                                        ALU.subtract, ALU.mult).then_inc(xn_ready, 1)

            def sums(n):
                v.wait_ge(x_in[n], 16)
                for t in range(*X_LOADS[n]):
                    ins = nc.vector.bn_stats(st[:, t, :], x_sb[:, t, :])
                link(ins)

            sums(0)
            statistics(0, 0, TB)
            for t in range(TB):
                normalise_x(bass.ds(t, 1))
            v.wait_ge(b_got, 16)
            link(nc.vector.tensor_copy(b_part[:, 0], b_in[:]))
            link(nc.vector.tensor_tensor(b_res[:], b_in[:], b_part[:, 0], ALU.subtract))
            link(nc.vector.tensor_copy(b_part[:, 1], b_res[:]))
            link(nc.vector.tensor_tensor(b_in[:], b_res[:], b_part[:, 1], ALU.subtract))
            nc.vector.tensor_copy(b_part[:, 2], b_in[:]).then_inc(b_done, 1)
            for n in range(1, len(X_LOADS)):
                sums(n)
            statistics(1, TB, NT)
            link(nc.vector.tensor_tensor(lw[:, 1], rstd[:, 0], rstd[:, 0], ALU.mult))
            link(nc.vector.tensor_tensor(lw[:, 2], lw[:, 1], lw[:, 5], ALU.mult))
            nc.vector.tensor_scalar(lw[:, 6], lw[:, 2], EPS_LN, None, ALU.add).then_inc(var_ready, 1)
            nc.vector.scalar_tensor_tensor(out=offset[:], in0=mean[:], scalar=-1.0, in1=rstd[:, 0],
                                           op0=ALU.mult, op1=ALU.mult).then_inc(mean_ready, 1)
            for t in range(TB, 2 * TB):
                normalise_x(bass.ds(t, 1))

            def map_experts():
                link(nc.vector.tensor_tensor(emap[:], tile_no[:].unsqueeze(2).to_broadcast([P, MAPPED, E]),
                                         ends[:].unsqueeze(1).to_broadcast([P, MAPPED, E]), ALU.is_ge))
                link(nc.vector.tensor_reduce(emap_f[:], emap[:], AX.X, ALU.add))
                nc.vector.tensor_scalar(emap_i[:], emap_f[:], float(E - 1), None, ALU.min).then_inc(map_ready, 1)

            def route(part):
                per_e = [P, NT, E]

                def bt(a):
                    return a.unsqueeze(2).to_broadcast(per_e)

                rev_b = rev[:].unsqueeze(1).to_broadcast(per_e)
                if part == 0:
                    v.wait_ge(gates_ready, B)
                    v.wait_ge(consts, 1)
                    nc.vector.tensor_copy(R["lg"], ps[:, 1, 0:NT * E].rearrange("p (t e) -> p t e", e=E)).then_inc(lg_out, 1)
                    v.wait_ge(lg_out, 1)
                    link(nc.vector.tensor_reduce(r1["m"][:], R["lg"], AX.X, ALU.max))
                    nc.vector.tensor_tensor(R["d"], R["lg"], bt(r1["m"][:]), ALU.subtract).then_inc(lg_d, 1)
                if part == 1:
                    v.wait_ge(lg_e, 1)
                    link(nc.vector.tensor_reduce(r1["s"][:], R["e"], AX.X, ALU.add))
                    link(nc.vector.reciprocal(r1["rs"][:], r1["s"][:]))
                    link(nc.vector.tensor_tensor(R["p"], R["e"], bt(r1["rs"][:]), ALU.mult))
                if part == 2:
                    link(nc.vector.tensor_reduce(r1["p1"][:], R["p"], AX.X, ALU.max))
                    link(nc.vector.tensor_tensor(R["key"], R["p"], bt(r1["p1"][:]), ALU.is_equal))
                    link(nc.vector.tensor_tensor(R["key"], R["key"], rev_b, ALU.mult))
                    link(nc.vector.tensor_reduce(r1["k1"][:], R["key"], AX.X, ALU.max))
                if part == 3:
                    link(nc.vector.tensor_tensor(R["oh1"], rev_b, bt(r1["k1"][:]), ALU.is_equal))
                    link(nc.vector.scalar_tensor_tensor(out=R["pm"], in0=R["oh1"], scalar=-2.0, in1=R["p"],
                                                        op0=ALU.mult, op1=ALU.add))
                    link(nc.vector.tensor_reduce(r1["p2"][:], R["pm"], AX.X, ALU.max))
                if part == 4:
                    link(nc.vector.tensor_tensor(R["key"], R["pm"], bt(r1["p2"][:]), ALU.is_equal))
                    link(nc.vector.tensor_tensor(R["key"], R["key"], rev_b, ALU.mult))
                    link(nc.vector.tensor_reduce(r1["k2"][:], R["key"], AX.X, ALU.max))
                if part == 5:
                    link(nc.vector.tensor_tensor(R["oh2"], rev_b, bt(r1["k2"][:]), ALU.is_equal))
                    nc.vector.tensor_tensor(ohb[:].rearrange("p e t -> p t e"), R["oh1"], R["oh2"], ALU.add).then_inc(oh_ready, 1)
                if part == 6:
                    link(nc.vector.scalar_tensor_tensor(out=r1["den"][:], in0=r1["p1"][:], scalar=EPS_TOPK, in1=r1["p2"][:],
                                                        op0=ALU.add, op1=ALU.add))
                    link(nc.vector.reciprocal(r1["rd"][:], r1["den"][:]))
                    link(nc.vector.tensor_tensor(zrow[:, :, D], r1["p1"][:], r1["rd"][:], ALU.mult))
                    link(nc.vector.tensor_tensor(w_late[:], r1["p2"][:], r1["rd"][:], ALU.mult))
                if part == 7:
                    v.wait_ge(counts_ready, 1)
                    nc.vector.tensor_copy(cnt[:], ps[:, 1, :].rearrange("p (a e t) -> p a e t", a=2, e=E)).then_inc(cnt_out, 1)
                    v.wait_ge(cnt_out, 1)
                    flat = "p e t -> p (e t)"
                    link(nc.vector.tensor_tensor_scan(cum[:].rearrange(flat), carry[:].rearrange(flat),
                                                      cnt[:, 1].rearrange(flat), 0.0, ALU.mult, ALU.add))
                    link(nc.vector.tensor_tensor(cmp[:], cum[:, :, NT - 1:NT].to_broadcast([P, E, NT]),
                                                 thr[:].unsqueeze(1).to_broadcast([P, E, NT]), ALU.is_gt))
                    link(nc.vector.tensor_reduce(ce[:], cmp[:], AX.X, ALU.add))
                if part == 8:
                    link(nc.vector.tensor_tensor_scan(ends[:], ones_b[:, 0:E], ce[:], 0.0, ALU.mult, ALU.add))
                    link(nc.vector.tensor_tensor(starts[:], ends[:], ce[:], ALU.subtract))
                    link(nc.vector.tensor_tensor(base[:], cum[:], cnt[:, 1], ALU.subtract))
                    link(nc.vector.tensor_tensor(base[:], base[:], cnt[:, 0], ALU.add))
                    link(nc.vector.scalar_tensor_tensor(out=base[:], in0=starts[:].unsqueeze(2).to_broadcast([P, E, NT]),
                                                        scalar=float(P), in1=base[:], op0=ALU.mult, op1=ALU.add))
                for c in range(2):
                    if part == 9 + c:
                        link(nc.vector.tensor_tensor(R["key"], R[f"oh{c + 1}"], base[:].rearrange("p e t -> p t e"), ALU.mult))
                        link(nc.vector.tensor_reduce(r1["slf"][:], R["key"], AX.X, ALU.add))
                        link(nc.vector.tensor_copy(slot[:, c], r1["slf"][:]))
                if part == 10:
                    v.sem_inc(slots_ready, 1)

            def values(b, u, quadrants):
                if quadrants:
                    v.wait_ge(v_ps, b + 1)
                for n in quadrants:
                    for c in range(4):
                        nc.vector.tensor_copy(v_diag(u, n, c), v_part(n, c)).then_inc(v_sb, 1)

            def first_queries():
                v.wait_ge(q_out, 1)
                v.wait_ge(masks, 1)
                for c in range(4):
                    nc.vector.tensor_scalar(qbd[:, 0, :, c, :], q_now[:].rearrange("p (n q) -> p n q", q=QB),
                                            qmask[:, c:c + 1], None, ALU.mult).then_inc(q_sb, 1)

            def maxima(b, j):
                v.wait_ge(s_ps, b * PAIRS + j + 1)
                nc.vector.tensor_reduce(negm[:, j % SR], ps[:, 2 + j % SR, :].rearrange("p (c k) -> p c k", k=2 * QB),
                                        AX.X, ALU.max, negate=True).then_inc(m_sb, 1)

            def turned_p(b, j):
                v.wait_ge(p_sb, 8 * (b * PAIRS + j + 1))
                nc.vector.transpose(pT[:, 2 * j:2 * j + 2, :].rearrange("p n c -> p (n c)"), pexp[:, j % SR]).then_inc(pT_sb, 1)

            def invert(b, half):
                if half == 0:
                    v.wait_ge(o_ps, b + 1)
                    wait(v, o_sb, b)
                at = slice(half * S // 2, (half + 1) * S // 2)
                nc.vector.reciprocal(rec[:, at], ps[:, 7, at]).then_inc(rec_sb, 1)

            def add(b, bank=1):
                v.wait_ge(a_ps, b + 1)
                v.wait_ge(x_plus, b + 1)
                xs = x_sb[:, bass.ds(b * TB, TB), :]
                nc.vector.tensor_tensor(xs, xs, ps[:, bank, :].rearrange("p (t d) -> p t d", t=TB), ALU.add).then_inc(a_sb, 1)

            def sequence(b, u, first, last, parts=()):
                for j in range(PAIRS):
                    if j >= TURN_LAG:
                        turned_p(b, j - TURN_LAG)
                    elif not first:
                        turned_p(b - 1, PAIRS + j - TURN_LAG)
                    maxima(b, j)
                    for part in range(2):
                        if j == DVE_V[part] and not last:
                            values(b + 1, 1 - u, range(ACT_QUADRANTS, 4)[part::2])
                        if j == DVE_INVERT[part] and not first:
                            invert(b - 1, part)
                    if j == DVE_ADD and not first:
                        add(b - 1)
                    if j < len(parts) and parts[j] is not None:
                        route(parts[j])

            first_queries()
            inverse_root(2, 1, 0, NT).then_inc(z_scale, 1)
            for t in range(2 * TB, LATE):
                normalise_x(bass.ds(t, 1))
            v.wait_ge(vbd_clear, 1)
            values(0, 0, range(2, 4))
            parts = [[None] * ROUTE_FROM + list(range(PAIRS - ROUTE_FROM)), list(range(PAIRS - ROUTE_FROM, PARTS))]
            sequence(0, 0, True, False, parts[0])
            sequence(1, 1, False, False, parts[1])
            with v.Fori(0, LOOPED) as i:
                for u in range(2):
                    sequence(2 + 2 * i + u, u, False, False)
            sequence(B - 2, 0, False, False)
            map_experts()
            sequence(B - 1, 1, False, True)
            for j in range(PAIRS - TURN_LAG, PAIRS):
                turned_p(B - 1, j)

            def turned_rows(turn, r):
                k = RING * turn + r
                v.wait_ge(xgT_ps, k + 1)
                wait(v, hT_ps, k - 1)
                nc.vector.tensor_scalar(xgT[:, r % 2], ps[:, 4 + r % 2, 0:P], cols[:, 2:3], cols[:, 3:4],
                                        ALU.mult, ALU.add).then_inc(xgT_sb, 1)

            expert = [v.alloc_register(f"expert{r}") for r in range(RING)]

            def load_experts(turn, half):
                v.load(expert[4 * half:4 * half + 4], emap_i[0:1, bass.ds(RING * turn + 4 * half, 4)])

            def set_weights(turn, r):
                k = RING * turn + r
                e = v.snap(expert[r], min_val=0, max_val=E - 1)
                wait(v, hT_sb, FC * (k - 1))
                nc.vector.tensor_copy(w1_now[:, r % 2], w1_sb[:, bass.ds(e, 1), :].rearrange("p a f -> p (a f)")).then_inc(w1_set, 1)

            def expert_step(turn, r):
                k = RING * turn + r
                if isinstance(k, int) and k >= SLOT_TILES - 1:
                    return
                turned_rows(turn + (r + 1) // RING, (r + 1) % RING)
                set_weights(turn + (r + 1) // RING, (r + 1) % RING)
                if r == 6:
                    load_experts(turn + 1, 1)
                if r == 2:
                    load_experts(turn + 1, 0)

            v.wait_ge(w1_in, 16)
            v.wait_ge(map_ready, 1)
            load_experts(0, 0)
            load_experts(0, 1)
            set_weights(0, 0)
            turned_rows(0, 0)
            run_experts(v, expert_step, ((INVERT_AT[0], lambda: invert(B - 1, 0)), (INVERT_AT[1], lambda: invert(B - 1, 1)),
                                         (ADD_AT, lambda: add(B - 1, 7))))
            for b in range(B):
                if b not in GPSIMD_SUMS:
                    v.wait_ge(y_got[b], 16)
                    xs, first_choice, second_choice = summands(b)
                    link(nc.vector.tensor_tensor(xs, xs, first_choice, ALU.add))
                    nc.vector.tensor_tensor(xs, xs, second_choice, ALU.add).then_inc(y_sum[b], 1)

        @block.tensor
        def _(pe):
            mm = nc.tensor.matmul

            def bias(dst, width, at, stop=False):
                return mm(dst, ones_b[0:3, :], b3[:, bass.ds(at, width)], start=True, stop=stop, skip_group_check=True)


            def turn_z(i):
                for b in (2 * i, 2 * i + 1):
                    pe.wait_ge(z_ready, b + 1)
                    for j in range(TB):
                        ins = nc.tensor.transpose(ps[:, 6 + b % 2, P * j:P * (j + 1)], z_now[:, b % 4, j, :], ident[:])
                    ins.then_inc(zT_ready, 1)

            def gates(i):
                for b in (2 * i, 2 * i + 1):
                    pe.wait_ge(xf_ready, b + 1)
                    for j in range(TB):
                        at = (b * TB + j) * E
                        ins = mm(ps[:, 1, at:at + E], xfT[:, b % 2, P * j:P * (j + 1)], wG[:], start=False, stop=(b == B - 1 and j == TB - 1),
                                 skip_group_check=True)
                    ins.then_inc(gates_ready, 1)

            def counts():
                pe.wait_ge(oh_ready, 1)
                pe.wait_ge(consts, 1)
                oh = ohb[:].rearrange("p e t -> p (e t)")
                mm(ps[:, 1, 0:E * NT], before[:], oh, start=True, stop=True, skip_group_check=True)
                mm(ps[:, 1, E * NT:2 * E * NT], ones_b[:], oh, start=True, stop=True, skip_group_check=True).then_inc(counts_ready, 1)

            pe.wait_ge(idents, 1)
            pe.wait_ge(w_in, 16)

            def turn_xn(b):
                pe.wait_ge(xnb_in, 16 * (b + 1))
                wait(pe, v_sb, 16 * b)
                for j in range(TB):
                    ins = nc.tensor.transpose(ps[:, 0, P * j:P * (j + 1)], xnb[:, j, :], ident[:])
                ins.then_inc(xnT_ps, 1)

            def project_v(b):
                pe.wait_ge(xnT_sb, b + 1)
                mm(ps[:, 0, :], ones_b[0:3, :], b3[:, O_BV:O_BV + D].unsqueeze(1).to_broadcast([3, TB, D]),
                   start=True, stop=False, skip_group_check=True)
                for j in range(TB):
                    ins = mm(ps[:, 0, D * j:D * (j + 1)], xnT[:, P * j:P * (j + 1)],
                             wA[:, 2, :], start=False, stop=(j == TB - 1), skip_group_check=True)
                ins.then_inc(v_ps, 1)

            def project_k(b):
                mm(ps[:, 1, :], wA[:, 1, :], xnT[:], start=True, stop=True).then_inc(k_ps, 1)

            def project_q(b, bank=0):
                if bank == 0:
                    pe.wait_ge(v_sb, 16 * (b + 1))
                mm(ps[:, bank, :], wA[:, 0, :], xnT[:], start=True, stop=True).then_inc(q_ps, 1)

            def scores(b, u, j):
                k = b * PAIRS + j
                wait(pe, p_sb, 8 * (k + 1 - SR))
                if j == 0:
                    if isinstance(b, int) and b == 0:
                        pe.wait_ge(masks, 1)
                    pe.wait_ge(k_sb, G * (b + 1))
                    pe.wait_ge(q_sb, 4 * (b + 1))
                first_pair = 0 if j == 0 else 1
                mm(ps[:, 2 + j % SR, :], identb[:], maskS[:, first_pair:first_pair + 2],
                   start=True, stop=False, skip_group_check=True)
                for n in range(2):
                    blk = 2 * j + n
                    ins = mm(ps[:, 2 + j % SR, 256 * n:256 * (n + 1)], qbd[:, u, blk].rearrange("p h q -> p (h q)"),
                             kz[:, u, :, QB * blk:QB * (blk + 2)], start=False, stop=(n == 1), skip_group_check=True)
                ins.then_inc(s_ps, 1)

            def values(u, m):
                wide = 2 if m < NQ - 1 else 1
                for g in range(G):
                    at = (m * 2 * G + 2 * g + 1) * QB
                    apart = (2 * G - 1) * QB
                    if wide == 2:
                        probs = flat_pT[:, at:at + 2 * apart].rearrange("p (a c) -> p a c", a=2)[:, :, 0:QB]
                    else:
                        probs = flat_pT[:, at:at + QB]
                    mm(ps[QB * g:QB * (g + 1), 6, QB * m:QB * (m + wide)], vbd[:, u, m, g, :], probs,
                       start=(m == 0), stop=(m == NQ - 1), skip_group_check=True)

            def denominators(half):
                n0 = half * NQ // 2
                for which in range(2):
                    for g in range(G):
                        ins = mm(ps[QB * g:QB * (g + 1), 7, QB * n0:QB * (n0 + NQ // 2)], vmask[:].rearrange("p h d -> p (h d)"),
                                 pT[:, n0:n0 + NQ // 2, (2 * g + which) * QB:(2 * g + which + 1) * QB],
                                 start=(half == 0 and which == 0), stop=(which == 1), skip_group_check=True)
                return ins

            def weigh(b, u, j):
                pe.wait_ge(pT_sb, b * PAIRS + j + 1)
                if j == 0:
                    wait(pe, o_out, b)
                    if isinstance(b, int) and b == 0:
                        pe.wait_ge(xf_ready, B)
                if j > 0:
                    values(u, 2 * j - 1)
                values(u, 2 * j)
                if j == PAIRS // 2:
                    wait(pe, rec_sb, 2 * b)
                    denominators(0)
                if j == PAIRS - 1:
                    values(u, NQ - 1)
                    denominators(1).then_inc(o_ps, 1)

            def project_out(b, bank=1):
                pe.wait_ge(o_sb, b + 1)
                mm(ps[:, bank, :], ones_b[0:3, :], b3[:, O_BO:O_BO + D].unsqueeze(1).to_broadcast([3, TB, D]),
                   start=True, stop=False, skip_group_check=True)
                for j in range(TB):
                    ins = mm(ps[:, bank, P * j:P * (j + 1)], attnT[:, P * j:P * (j + 1)], wA[:, 3, :],
                             start=False, stop=(j == TB - 1), skip_group_check=True)
                ins.then_inc(a_ps, 1)

            def sequence(b, u, first, last):
                second = isinstance(b, int) and b == 1
                for j in range(PAIRS):
                    scores(b, u, j)
                    if first and j == 0:
                        pe.wait_ge(wG_in, 16)
                        mm(ps[:, 1, 0:NT * E], ones_b[0:3, :], b3[:, O_BG:O_BG + E].unsqueeze(1).to_broadcast([3, NT, E]),
                           start=True, stop=False, skip_group_check=True)
                    if first and 1 <= j <= B // 2:
                        gates(j - 1)
                    if first and j < B // 2:
                        turn_z(j)
                    if j >= WEIGH_LAG:
                        weigh(b, u, j - WEIGH_LAG)
                    elif not first:
                        weigh(b - 1, 1 - u, PAIRS + j - WEIGH_LAG)
                    if second and j == COUNTS_AT:
                        counts()
                    if not last:
                        if j == PE_XN:
                            turn_xn(b + 1)
                        if j == PE_V:
                            project_v(b + 1)
                        if j == PE_K:
                            if first:
                                pe.wait_ge(lg_out, 1)
                            if second:
                                pe.wait_ge(cnt_out, 1)
                            project_k(b + 1)
                        if j == PE_Q:
                            project_q(b + 1)
                    if j == PE_OUT and not first:
                        if not last:
                            pe.wait_ge(k_sb, G * (b + 2))
                        project_out(b - 1)

            turn_xn(0)
            pe.wait_ge(xnT_sb, 1)
            project_q(0, 4)
            project_k(0)
            pe.wait_ge(b3_in, 16)
            project_v(0)
            sequence(0, 0, True, False)
            sequence(1, 1, False, False)
            with pe.Fori(0, LOOPED) as i:
                for u in range(2):
                    sequence(2 + 2 * i + u, u, False, False)
            sequence(B - 2, 0, False, False)
            sequence(B - 1, 1, False, True)
            for j in range(PAIRS - WEIGH_LAG, PAIRS):
                weigh(B - 1, 1, j)
            pe.wait_ge(w2_in, 16)
            pe.wait_ge(a_sb, B - 1)

            def turn_rows(turn, r):
                k = RING * turn + r
                pe.wait_ge(xg_in[r], 16 * (turn + 1))
                wait(pe, xgT_sb, k - 1)
                nc.tensor.transpose(ps[:, 4 + r % 2, 0:P], xg[:, r, 0:D], ident[:]).then_inc(xgT_ps, 1)

            expert = [pe.alloc_register(f"expert{r}") for r in range(RING)]

            def load_experts(turn, half):
                pe.load(expert[4 * half:4 * half + 4], emap_i[0:1, bass.ds(RING * turn + 4 * half, 4)])

            def expert_step(turn, r):
                k = RING * turn + r
                start, last = (isinstance(k, int) and k == n for n in (0, SLOT_TILES))
                if not last:
                    if not (isinstance(k, int) and k == SLOT_TILES - 1):
                        turn_rows(turn + (r + 1) // RING, (r + 1) % RING)
                    pe.wait_ge(xgT_sb, k + 1)
                    pe.wait_ge(w1_set, k + 1)
                    wait(pe, hT_sb, FC * (k - 1))
                    for c in range(FC):
                        ins = mm(ps[:, r % 2, P * c:P * (c + 1)], w1_now[:, r % 2, P * c:P * (c + 1)], xgT[:, r % 2, :],
                                 start=True, stop=True, skip_group_check=True)
                    ins.then_inc(hT_ps, 1)
                if not start:
                    before = (r - 1) % RING
                    e = pe.snap(expert[before], min_val=0, max_val=E - 1)
                    wait(pe, y_sb, k - 2)
                    bias(ps[:, 2 + before % 2, 0:D], D, e * D + O_B2)
                    pe.wait_ge(hT_sb, FC * k)
                    for c in range(FC):
                        ins = mm(ps[:, 2 + before % 2, 0:D], hT[:, before % 2, c, :],
                                 w2_sb[:, bass.ds(e * FC + c, 1), :], start=False, stop=(c == FC - 1), skip_group_check=True)
                    ins.then_inc(y_ps, 1)
                    if r == 0:
                        load_experts(turn, 1)
                    if r == 4:
                        load_experts(turn + 1, 0)

            pe.wait_ge(map_ready, 1)
            load_experts(0, 0)
            load_experts(0, 1)
            turn_rows(0, 0)
            run_experts(pe, expert_step, ((OUT_AT, lambda: project_out(B - 1, 7)),))


def kernel(**inputs):
    import numpy as np
    import concourse.bacc as bacc
    from concourse.bass_utils import run_bass_kernel_spmd

    a = {k[3:]: np.asarray(v) for k, v in inputs.items()}
    E, DF, D = a["ffn_W1"].shape
    w_attn = np.stack([a["attn_W" + n].T for n in "qkvo"], axis=1)
    b_cols = np.stack([a["attn_bq"], a["attn_bk"], a["ffn_gamma"], a["ffn_beta"]], axis=1)
    rows = np.concatenate([a["ffn_b2"].ravel(), a["attn_bo"], a["attn_bv"], a["ffn_bg"]])
    width = -(-rows.size // 128) * 128
    bias_rows = np.zeros((1, width), rows.dtype)
    bias_rows[0, :rows.size] = rows
    w1 = np.concatenate([a["ffn_W1"].transpose(2, 0, 1), a["ffn_b1"].reshape(E, DF // 128, 128).transpose(2, 0, 1)], axis=2)
    w2 = a["ffn_W2"].transpose(2, 0, 1).reshape(DF // 128, 128, E, D).transpose(1, 2, 0, 3).reshape(128, E * (DF // 128), D)
    ins = {"x": a["attn_x"], "w_attn": w_attn, "b_cols": b_cols, "bias_rows": bias_rows,
           "w_gate": a["ffn_Wg"].T, "w1": w1, "w2": w2}
    ins = {k: np.ascontiguousarray(v) for k, v in ins.items()}

    nc = bacc.Bacc("TRN2", target_bir_lowering=False, num_devices=1)
    args = [nc.dram_tensor("in_" + k, v.shape, F32, kind="ExternalInput").ap() for k, v in ins.items()]
    out = nc.dram_tensor("out", a["attn_x"].shape, F32, kind="ExternalOutput").ap()
    attention_and_experts(nc, *args, out)
    got = run_bass_kernel_spmd(nc, [{"in_" + k: v for k, v in ins.items()}], core_ids=[0])
    return got.results[0]["out"]
```
